# Optimizing a Trainium2 kernel written in Bass

```python
import numpy as np
import jax
import jax.numpy as jnp

def _softmax(x, axis=-1):
    return jax.nn.softmax(x, axis=axis)

def _gelu(x):
    return jax.nn.gelu(x, approximate=True)

def _silu(x):
    return jax.nn.silu(x)

def _sigmoid(x):
    return jax.nn.sigmoid(x)

def _layernorm(x, axis=-1, eps=1e-05):
    m = jnp.mean(x, axis=axis, keepdims=True)
    v = jnp.var(x, axis=axis, keepdims=True)
    return (x - m) / jnp.sqrt(v + eps)

def _scatter_add(tgt, idx, src, axis=0):
    return tgt.at[idx].add(src)

def _segment_sum(src, seg, n):
    return jax.ops.segment_sum(src, seg, n)
kernel_name = 'mk_adaln_d1_jaxref_r8_b87bcb'

def setup_inputs(seed: int=0):
    np.random.seed(seed)
    _w = jnp.asarray

    def _L0_attn_setup():
        import jax, jax.numpy as jnp
        import numpy as np
        NHEAD = 8
        ATTN_EPS = 1e-06
        LN_EPS = 1e-05

        def _layernorm(y, g, b):
            mu = jnp.mean(y, axis=-1, keepdims=True)
            var = jnp.var(y, axis=-1, keepdims=True)
            return (y - mu) * jax.lax.rsqrt(var + LN_EPS) * g + b
        key = jax.random.key(seed)
        ks = jax.random.split(key, 6)
        B, L, D = (2, 1024, 128)
        s = 1.0 / np.sqrt(D)
        return {'x': jax.random.normal(ks[0], (B, L, D), jnp.float32), 'Wq': jax.random.normal(ks[1], (D, D), jnp.float32) * s, 'Wm': jax.random.normal(ks[2], (D, D), jnp.float32) * s, 'W1': jax.random.normal(ks[3], (D, 2 * D), jnp.float32) * s, 'W2': jax.random.normal(ks[4], (2 * D, D), jnp.float32) * (1.0 / np.sqrt(2 * D)), 'g1': jnp.ones((D,), jnp.float32), 'b1': jnp.zeros((D,), jnp.float32), 'g2': jnp.ones((D,), jnp.float32), 'b2': jnp.zeros((D,), jnp.float32)}
    _L0_attn_in = _L0_attn_setup()

    def _L0_ffn_setup():
        import jax, jax.numpy as jnp
        import numpy as np
        key = jax.random.key(seed)
        k0, k1, k2, k3 = jax.random.split(key, 4)
        B, S, D, F, E = (8, 256, 128, 256, 8)
        x = jax.random.normal(k0, (B, S, D), dtype=jnp.float32)
        Wg = jax.random.normal(k1, (D, E), dtype=jnp.float32) * 0.02
        W1 = jax.random.normal(k2, (E, D, F), dtype=jnp.float32) * 0.02
        W2 = jax.random.normal(k3, (E, F, D), dtype=jnp.float32) * 0.02
        return {'x': x, 'Wg': Wg, 'W1': W1, 'W2': W2}
    _L0_ffn_in = _L0_ffn_setup()
    _L0_c = _w((lambda *s: np.random.randn(*s).astype(np.float32) * 0.05)(2, 128))
    _L0_wmod = _w((lambda *s: np.random.randn(*s).astype(np.float32) * 0.05)(128, 6 * 128) * 128 ** (-0.5))
    _d = {'L0_attn_x': _L0_attn_in['x'], 'L0_attn_Wq': _L0_attn_in['Wq'], 'L0_attn_Wm': _L0_attn_in['Wm'], 'L0_attn_W1': _L0_attn_in['W1'], 'L0_attn_W2': _L0_attn_in['W2'], 'L0_attn_g1': _L0_attn_in['g1'], 'L0_attn_b1': _L0_attn_in['b1'], 'L0_attn_g2': _L0_attn_in['g2'], 'L0_attn_b2': _L0_attn_in['b2'], 'L0_ffn_Wg': _L0_ffn_in['Wg'], 'L0_ffn_W1': _L0_ffn_in['W1'], 'L0_ffn_W2': _L0_ffn_in['W2'], 'L0_c': _L0_c, 'L0_wmod': _L0_wmod}
    _x0 = _d['L0_attn_x']
    _d['L0_attn_x'] = jax.random.normal(jax.random.fold_in(jax.random.key(seed), 1), (2, 2048, 128), dtype=_x0.dtype)
    del _x0
    return _d

def reference(L0_attn_x, L0_attn_Wq, L0_attn_Wm, L0_attn_W1, L0_attn_W2, L0_attn_g1, L0_attn_b1, L0_attn_g2, L0_attn_b2, L0_ffn_Wg, L0_ffn_W1, L0_ffn_W2, L0_c, L0_wmod):

    def _L0_attn_ref(x, Wq, Wm, W1, W2, g1, b1, g2, b2):
        import jax, jax.numpy as jnp
        import numpy as np
        NHEAD = 8
        ATTN_EPS = 1e-06
        LN_EPS = 1e-05

        def _layernorm(y, g, b):
            mu = jnp.mean(y, axis=-1, keepdims=True)
            var = jnp.var(y, axis=-1, keepdims=True)
            return (y - mu) * jax.lax.rsqrt(var + LN_EPS) * g + b
        B, L, D = x.shape
        H = NHEAD
        d = D // H
        q = (x @ Wq).reshape(B, L, H, d)
        feat = jax.nn.elu(q) + 1.0
        Q = feat
        K = feat
        V = q / L
        KV = jnp.einsum('nshd,nshv->nhdv', K, V)
        Ksum = K.sum(axis=1)
        Z = 1.0 / (jnp.einsum('nlhd,nhd->nlh', Q, Ksum) + ATTN_EPS)
        msg = jnp.einsum('nlhd,nhdv,nlh->nlhv', Q, KV, Z) * L
        msg = msg.reshape(B, L, D) @ Wm
        x = x + _layernorm(msg, g1, b1)
        mlp = jax.nn.relu(msg @ W1) @ W2
        x = x + _layernorm(mlp, g2, b2)
        return x

    def _L0_ffn_ref(x, Wg, W1, W2):
        import jax, jax.numpy as jnp
        import numpy as np
        B, S, D = x.shape
        E = Wg.shape[1]
        T = B * S
        cap = max(1, T // E)
        xt = x.reshape(T, D)
        logits = xt @ Wg
        probs = jax.nn.softmax(logits, axis=-1)
        pT = probs.T
        _, top_idx = jax.lax.top_k(pT, cap)
        sel = jnp.zeros((E, T), dtype=bool).at[jnp.arange(E)[:, None], top_idx].set(True)
        masked = jnp.where(sel, pT, -jnp.inf)
        assigned = sel.any(axis=0)
        tok2exp = jnp.where(assigned, jnp.argmax(masked, axis=0), jnp.argmax(pT, axis=0))
        weights = jnp.take_along_axis(probs, tok2exp[:, None], axis=1)[:, 0]
        out = jnp.zeros_like(xt)
        for e in range(E):
            gate = jnp.where(tok2exp == e, weights, 0.0)
            h = jax.nn.gelu(xt @ W1[e], approximate=False) @ W2[e]
            out = out + gate[:, None] * h
        return out.reshape(B, S, D)
    x = L0_attn_x
    mod = (_silu(L0_c) @ L0_wmod).reshape(L0_c.shape[0], 6, 1, -1)
    sa, ca, ga, sb, cb, gb = (mod[:, 0], mod[:, 1], mod[:, 2], mod[:, 3], mod[:, 4], mod[:, 5])
    ga = (2 * (ga >= 0) - 1) * jnp.maximum(jnp.abs(ga), 0.25)
    gb = (2 * (gb >= 0) - 1) * jnp.maximum(jnp.abs(gb), 0.25)
    h = _layernorm(x, axis=-1) * (1 + ca) + sa
    x = x + ga * _L0_attn_ref(h, L0_attn_Wq, L0_attn_Wm, L0_attn_W1, L0_attn_W2, L0_attn_g1, L0_attn_b1, L0_attn_g2, L0_attn_b2)
    h = _layernorm(x, axis=-1) * (1 + cb) + sb
    x = x + gb * _L0_ffn_ref(h, L0_ffn_Wg, L0_ffn_W1, L0_ffn_W2)
    return x

_drawn_inputs = setup_inputs


def setup_inputs(seed=0):
    import zlib

    import numpy as np

    out = dict(_drawn_inputs(seed))
    spreads = {'L0_attn_g1': (1.0, 0.2),
     'L0_attn_b1': (0.0, 0.334),
     'L0_attn_g2': (1.0, 0.2),
     'L0_attn_b2': (0.0, 0.332)}
    factors = {'L0_ffn_Wg': 8.0, 'L0_ffn_W1': 8.0, 'L0_ffn_W2': 8.0}
    for name, (base, spread) in spreads.items():
        noise = np.random.default_rng([zlib.crc32(name.encode()), seed]).standard_normal(out[name].shape)
        drawn = base * np.exp(spread * noise) if base else spread * noise
        out[name] = jnp.asarray(drawn.astype(out[name].dtype))
    for name, factor in factors.items():
        out[name] = (out[name] * factor).astype(out[name].dtype)
    return out
```

```python
from contextlib import ExitStack

import concourse.bass as bass
from concourse import mybir

F32 = mybir.dt.float32
BF16 = mybir.dt.bfloat16
I32 = mybir.dt.int32
ALU = mybir.AluOpType
ACT = mybir.ActivationFunctionType
AX = mybir.AxisListType

P = 128
B, L, D = 2, 2048, 128
H, HD = 8, 16
E, F = 8, 256
CAP = B * L // E
TB = L // P
NT = B * TB
GT = 4
G = NT // GT
GB = G // B
W = GT * P
LN_EPS = 1e-5
ATTN_EPS = 1e-6
HI_SHIFT = 14
HI_ROUNDS, LO_ROUNDS = 8, 7


def build(nc, x, Wq, Wm, W1, W2, g1, b1, g2, b2, Wg, EW1, EW2, c, wmod, out):
    with ExitStack() as ctx:
        def sb(name, shape, dt=F32):
            return ctx.enter_context(nc.sbuf_tensor(name, shape, dt))

        def psum(name):
            return ctx.enter_context(nc.psum_tensor(name, [P, 512], F32))

        def sem(name):
            return ctx.enter_context(nc.semaphore(name))

        x_sb = sb("x_sb", [P, NT, D])
        featT = sb("featT", [P, NT * P])
        feat = sb("feat", [P, NT, D])
        h2T = sb("h2T", [P, NT * P])
        ew1 = sb("ew1", [P, E, F])
        ew2 = sb("ew2", [P, E, 2, D])

        wq = sb("wq", [P, D]); wm = sb("wm", [P, D]); w1 = sb("w1", [P, F]); w2 = sb("w2", [P, 2, D])
        wg = sb("wg", [P, E]); wmod_sb = sb("wmod_sb", [P, 6 * D]); cT = sb("cT", [P, B])
        rows = sb("rows", [P, 4, D])
        wmT = sb("wmT", [P, D])
        wmx = sb("wmx", [P, D + F])
        wqm = sb("wqm", [P, B, D])
        qbias = sb("qbias", [P, B, D])

        ident = sb("ident", [P, P]); ones = sb("ones", [P, P]); same16 = sb("same16", [P, P])
        before = sb("before", [P, P], BF16); onesb = sb("onesb", [P, P], BF16)
        neghalf = sb("neghalf", [P, 8]); steps = sb("steps", [P, 12]); jc = sb("jc", [P, 4])
        eidx = sb("eidx", [P, E]); segmask = sb("segmask", [P, NT * E])

        ec = sb("ec", [P, B]); siluT = sb("siluT", [P, B]); siluB = sb("siluB", [P, B, P])
        colm = sb("colm", [P, 4, B])
        saB = sb("saB", [P, B, P])
        gaR = sb("gaR", [P, B, D]); gbR = sb("gbR", [P, B, D]); sgn = sb("sgn", [P, D])
        rA = sb("rA", [P, B, D]); rB = sb("rB", [P, B, D]); rC = sb("rC", [P, B, D]); rD = sb("rD", [P, B, D])
        bsum = sb("bsum", [P, D]); rowm = sb("rowm", [P, 4])

        bn = sb("bn", [P, 2, GT, 6]); mv = sb("mv", [P, 2, GT, 2]); ve = sb("ve", [P, 2, GT]); rs = sb("rs", [P, 2, GT])
        xn = sb("xn", [P, 4, GT, D]); hT = sb("hT", [P, 2, W]); ex = sb("ex", [P, 2, W])
        ksp = sb("ksp", [P, G]); ksum = sb("ksum", [P, B]); ksel = sb("ksel", [P, B, H]); kdiag = sb("kdiag", [P, B, P])
        gts = sb("gts", [P, B, P]); kvt = sb("kvt", [P, B, P]); mall = sb("mall", [P, B, D + F])
        z = sb("z", [P, 2, GT * H]); qp = sb("qp", [P, 2, W]); qT = sb("qT", [P, 2, W])
        hid = sb("hid", [P, 2, 2, W]); ssq = sb("ssq", [P, 2, 2 * GT]); yv = sb("yv", [P, 2, 2 * GT]); yr = sb("yr", [P, 2, 2 * GT])
        u1 = sb("u1", [P, 2, GT, D]); u2 = sb("u2", [P, GT, D]); t1 = sb("t1", [P, GT, D]); sqj = sb("sqj", [P, 2, 2 * GT, D], BF16)

        mx = sb("mx", [P, B, TB]); pr = sb("pr", [P, B, E, TB]); pe_ = sb("pe_", [P, B, E, TB]); sm = sb("sm", [P, B, TB])
        prT = sb("prT", [P, B * P]); khi = sb("khi", [P, B * P]); ki = sb("ki", [P, B * P], I32); klo = sb("klo", [P, B * P])
        junk = sb("junk", [P, 3, B * P], BF16); cur = sb("cur", [P, 2, 4]); pre = sb("pre", [P, 4]); cnt = sb("cnt", [P, 3]); dig = sb("dig", [P, 3])
        digit = sb("digit", [P, 1]); thi = sb("thi", [P, 2], I32); thd = sb("thd", [P, P]); thr = sb("thr", [P, P])
        gt_b = sb("gt_b", [P, B, E, TB], BF16); eq = sb("eq", [P, B, E, TB]); scan = sb("scan", [P, B, E, TB])
        rsum = sb("rsum", [P, B, E], BF16); base = sb("base", [P, B, E]); cgt = sb("cgt", [P, E])
        sel = sb("sel", [P, B, E, TB]); m1 = sb("m1", [P, B, E, TB]); m2 = sb("m2", [P, B, E, TB]); anys = sb("anys", [P, B, TB])
        gate = sb("gate", [P, NT, E])

        eh = sb("eh", [P, 2, 2, W]); ya = sb("ya", [P, GT, D])

        pT, pF, pQ0, pQ1, pH0, pH1, pG, pL = (psum(n) for n in ("pT", "pF", "pQ0", "pQ1", "pH0", "pH1", "pG", "pL"))
        pQ, pH, pGL = (pQ0, pQ1), (pH0, pH1), (pG, pL)

        names = """ld_mod ld_attn ld_moe consts
            silu_exp silu_done mod_cols cols_ready mod_rows rows_read wmT_ready wmT_done wmw1_ready wmx_done qb_ready prep_done rows_done
            stats1 rs1 xn1 tx hT_done q_ready exp_done feat_done tf ft_done gt_done acc_done
            ks_done gts_done kv_ready kvt_done mall_ready mall_done
            den_ready z_done qp_done tq qT_done y1_ready m1_ready relu0 relu1 y2_ready sq1 sq2 u1_done u2_done yr_done x1_done
            stats3 rs3 xn3 tx3 h2_done lg_ready
            lmax exp2 probs prt_ready counts totals keys diagT thr_ready gt_ready cgt_ready rsum_ready base_ready route_done
            eh_ready eh_done ey_ready ey_free gated digits o_done o_stored dve pool""".split()
        S = {n: sem(n) for n in names}
        ld_x = [sem(f"ld_x{g}") for g in range(G)]

        block = ctx.enter_context(nc.Block())

        def bgroup(t, g):
            return t[:, g * GT:(g + 1) * GT, :]

        def row4(r):
            return r.unsqueeze(1).to_broadcast([P, GT, D])

        @block.sync
        def _(sp):
            xv = x.rearrange("b (p t) d -> b p t d", p=P)
            sp.dma_start(wmod_sb[:, :], wmod).then_inc(S["ld_mod"], 16)
            for g in range(G):
                t0 = g % GB * GT
                sp.dma_start(bgroup(x_sb, g), xv[g // GB, :, t0:t0 + GT, :]).then_inc(ld_x[g], 16)
                if g == 0:
                    sp.dma_start(wq[:, :], Wq).then_inc(S["ld_attn"], 16)
                    sp.dma_start(wm[:, :], Wm).then_inc(S["ld_attn"], 16)
                    sp.dma_start(w1[:, :], W1).then_inc(S["ld_attn"], 16)
                    sp.dma_start(w2[:, :, :], W2.rearrange("(k p) d -> p k d", p=P)).then_inc(S["ld_attn"], 16)
                    sp.dma_start(wg[:, :], Wg).then_inc(S["ld_attn"], 16)
                    for n, r in enumerate((g1, b1, g2, b2)):
                        sp.dma_start(rows[:, n, :], r.partition_broadcast(P)).then_inc(S["ld_attn"], 16)
            sp.dma_start(ew1[:, :, :], EW1.rearrange("e d f -> d e f")).then_inc(S["ld_moe"], 16)
            sp.dma_start(ew2[:, :, :, :], EW2.rearrange("e (k p) d -> p e k d", p=P)).then_inc(S["ld_moe"], 16)
            ov = out.rearrange("b (p t) d -> b p t d", p=P)
            for g in range(G):
                t0 = g % GB * GT
                sp.wait_ge(S["o_done"], g + 1)
                sp.dma_start(ov[g // GB, :, t0:t0 + GT, :], bgroup(x_sb, g)).then_inc(S["o_stored"], 16)
            sp.wait_ge(S["o_stored"], 16 * G)

        @block.gpsimd
        def _(gp):
            n = 0

            def link(ins):
                nonlocal n
                n += 1
                ins.then_inc(S["pool"], 1)
                gp.wait_ge(S["pool"], n)

            gp.memset(ident[:, :], 0.0)
            gp.memset(ones[:, :], 1.0)
            gp.memset(onesb[:, :], 1.0)
            gp.memset(same16[:, :], 1.0)
            gp.memset(before[:, :], 1.0)
            gp.memset(neghalf[:, :], -0.5)
            gp.memset(segmask[:, :], 1.0)
            for k in range(9):
                gp.memset(steps[:, k:k + 1], float(4.0 ** (7 - k)))
            for k in range(4):
                gp.memset(jc[:, k:k + 1], float(k))
            link(gp.memset(rowm[:, 0:1], 0.0))
            gp.affine_select(out=ident[:, :], in_=ident[:, :], compare_op=ALU.not_equal, fill=1.0, base=0,
                             pattern=[[-1, P]], channel_multiplier=1)
            gp.affine_select(out=before[:, :], in_=before[:, :], compare_op=ALU.is_gt, fill=0.0, base=0,
                             pattern=[[1, P]], channel_multiplier=-1)
            gp.affine_select(out=segmask[:, :], in_=segmask[:, :], compare_op=ALU.not_equal, fill=0.0, base=0,
                             pattern=[[0, B * E], [1, TB]], channel_multiplier=0)
            gp.iota(eidx[:, :], pattern=[[1, E]], base=0, channel_multiplier=0, allow_small_or_imprecise_dtypes=True)
            sv = same16[:, :].rearrange("p (h c) -> p h c", c=HD)
            link(gp.affine_select(out=sv, in_=sv, compare_op=ALU.is_ge, fill=0.0, base=0,
                                  pattern=[[-HD, H], [0, HD]], channel_multiplier=1))
            gp.affine_select(out=sv, in_=sv, compare_op=ALU.is_ge, fill=0.0, base=HD - 1,
                             pattern=[[HD, H], [0, HD]], channel_multiplier=-1).then_inc(S["consts"], 1)

            def rsqrt(dst, src, tmp, scale, eps, width):
                link(gp.tensor_scalar(tmp, src, scale, eps, ALU.mult, ALU.add))
                return gp.tensor_tensor(dst, tmp, neghalf[:, 0:width], ALU.pow)

            def rs_a(g):
                gp.wait_ge(S["stats1"], g + 1)
                rsqrt(rs[:, g % 2, :], mv[:, g % 2, :, 1], ve[:, g % 2, :], 1.0, LN_EPS, GT).then_inc(S["rs1"], 1)

            def acc(g):
                b = g // GB
                gp.wait_ge(S["xn1"], g + 1)
                if g:
                    gp.wait_ge(S["acc_done"], g)
                link(gp.tensor_tensor(t1[:, :, :], xn[:, g % 4], row4(rA[:, b, :]), ALU.mult))
                link(gp.tensor_tensor(t1[:, :, :], t1[:, :, :], row4(rD[:, b, :]), ALU.add))
                gp.tensor_tensor(bgroup(x_sb, g), bgroup(x_sb, g), t1[:, :, :], ALU.add).then_inc(S["acc_done"], 1)

            rs_a(0)
            for g in range(G):
                if g + 1 < G:
                    rs_a(g + 1)
                if g == 0:
                    gp.wait_ge(S["rows_done"], 1)
                acc(g)

            def qprime(g):
                gp.wait_ge(S["z_done"], g + 1)
                if g >= 2:
                    gp.wait_ge(S["tq"], g - 1)
                gp.wait_ge(S["ft_done"], g + 1)
                gp.tensor_tensor(qp[:, g % 2, :].rearrange("p (t c) -> p t c", c=HD),
                                 bgroup(feat, g).rearrange("p t (h c) -> p (t h) c", c=HD),
                                 z[:, g % 2, :].unsqueeze(2).to_broadcast([P, GT * H, HD]), ALU.mult).then_inc(S["qp_done"], 1)

            for s in range(G + 4):
                if s < G:
                    qprime(s)
                g = s - 3
                if 0 <= g < G:
                    gp.wait_ge(S["sq1"], g + 1)
                    gp.wait_ge(S["sq2"], g + 1)
                    if g >= 2:
                        gp.wait_ge(S["x1_done"], g - 1)
                    rsqrt(yr[:, g % 2, :], ssq[:, g % 2, :], yv[:, g % 2, :], 1.0 / D, LN_EPS, 2 * GT).then_inc(S["yr_done"], 1)
                    gp.wait_ge(S["stats3"], g + 1)
                    rsqrt(rs[:, g % 2, :], mv[:, g % 2, :, 1], ve[:, g % 2, :], 1.0, LN_EPS, GT).then_inc(S["rs3"], 1)

        @block.scalar
        def _(act):
            n = 0
            act.dma_start(cT[:, :], c.rearrange("b d -> d b"), allow_slow_non_contiguous=True).then_inc(S["ld_mod"], 16)
            act.wait_ge(S["ld_mod"], 32)
            act.activation(ec[:, :], cT[:, :], ACT.Exp, scale=-1.0).then_inc(S["silu_exp"], 1)
            act.wait_ge(S["cols_ready"], 1)

            def a_hT(g):
                b = g // GB
                act.wait_ge(S["tx"], g + 1)
                if g >= 2:
                    act.wait_ge(S["q_ready"], g - 1)
                act.activation(hT[:, g % 2, :], pT[:, :], ACT.Identity, bias=colm[:, 0, b:b + 1],
                               scale=colm[:, 1, b:b + 1]).then_inc(S["hT_done"], 1)

            def a_exp(g):
                act.wait_ge(S["q_ready"], g + 1)
                if g >= 2:
                    act.wait_ge(S["feat_done"], g - 1)
                act.activation(ex[:, g % 2, :], pQ[g % 2][:, :], ACT.Exp).then_inc(S["exp_done"], 1)

            def a_ft(g):
                act.wait_ge(S["tf"], g + 1)
                act.copy(bgroup(feat, g), pF[:, :].rearrange("p (t d) -> p t d", d=D)).then_inc(S["ft_done"], 1)

            def a_kv(b):
                act.wait_ge(S["gt_done"], GB * (b + 1))
                act.copy(gts[:, b, :], pGL[b][:, 0:P]).then_inc(S["gts_done"], 1)
                act.wait_ge(S["mall_ready"], b + 1)
                act.copy(mall[:, b, :], pH1[:, 0:D + F]).then_inc(S["mall_done"], 1)

            for s in range(G + 3):
                if s < G:
                    a_hT(s)
                if 0 <= s - 1 < G:
                    a_exp(s - 1)
                if 0 <= s - 2 < G:
                    a_ft(s - 2)
                if s == GB + 3:
                    a_kv(0)
            a_kv(1)

            def a_qT(g):
                act.wait_ge(S["tq"], g + 1)
                if g >= 2:
                    act.wait_ge(S["m1_ready"], g - 1)
                act.copy(qT[:, g % 2, :], pF[:, :]).then_inc(S["qT_done"], 1)

            def a_relu(g):
                act.wait_ge(S["m1_ready"], g + 1)
                if g >= 2:
                    act.wait_ge(S["y2_ready"], g - 1)
                act.activation(hid[:, g % 2, 0, :], pH0[:, :], ACT.Relu).then_inc(S["relu0"], 1)

            def a_square(g, k, ready, done):
                act.wait_ge(S[ready], g + 1)
                if g >= 2:
                    act.wait_ge(S["yr_done"], g - 1)
                for t in range(GT):
                    last = act.activation(sqj[:, g % 2, k * GT + t, :], pQ[k][:, t * D:(t + 1) * D], ACT.Square,
                                          accum_out=ssq[:, g % 2, k * GT + t:k * GT + t + 1])
                last.then_inc(S[done], 1)

            def a_h2(g):
                b = g // GB
                act.wait_ge(S["tx3"], g + 1)
                act.activation(h2T[:, g * W:(g + 1) * W], pT[:, :], ACT.Identity, bias=colm[:, 2, b:b + 1],
                               scale=colm[:, 3, b:b + 1]).then_inc(S["h2_done"], 1)

            for s in range(G + 6):
                if 0 <= s - 1 < G:
                    a_qT(s - 1)
                if 0 <= s - 2 < G:
                    a_square(s - 2, 0, "y1_ready", "sq1")
                    a_relu(s - 2)
                if 0 <= s - 3 < G:
                    a_square(s - 3, 1, "y2_ready", "sq2")
                if 0 <= s - 5 < G:
                    a_h2(s - 5)
            act.wait_ge(S["lmax"], 1)
            act.activation(pe_[:, :, :, :].rearrange("p b e t -> p (b e t)"), m1[:, :, :, :].rearrange("p b e t -> p (b e t)"),
                           ACT.Exp).then_inc(S["exp2"], 1)
            with act.Fori(0, G * E // 2) as i:
                for k in range(2):
                    for f in range(2):
                        act.wait_ge(S["eh_ready"], i * 4 + (2 * k + f + 1))
                        act.activation(eh[:, k, f, :], (pH if k == 0 else pQ)[f][:, :], ACT.Gelu).then_inc(S["eh_done"], 1)

        @block.tensor
        def _(te):
            te.wait_ge(S["consts"], 1)
            te.wait_ge(S["silu_done"], 1)
            te.wait_ge(S["ld_mod"], 32)
            for n, j in enumerate((0, 1, 3, 4)):
                mm = te.matmul(pG[:, 2 * n:2 * n + 2], wmod_sb[:, j * D:(j + 1) * D], siluT[:, :], start=True, stop=True)
            mm.then_inc(S["mod_cols"], 1)
            te.wait_ge(S["silu_done"], 2)

            def p_tx(g):
                te.wait_ge(S["xn1"], g + 1)
                if g >= 1:
                    te.wait_ge(S["hT_done"], g)
                for t in range(GT):
                    mm = te.transpose(pT[:, t * P:(t + 1) * P], xn[:, g % 4, t, :], ident[:, :])
                mm.then_inc(S["tx"], 1)

            def p_q(g):
                te.wait_ge(S["hT_done"], g + 1)
                if g >= 2:
                    te.wait_ge(S["feat_done"], g - 1)
                te.matmul(pQ[g % 2][:, :], wq[:, :], hT[:, g % 2, :], start=True, stop=True).then_inc(S["q_ready"], 1)

            def p_tf(g):
                te.wait_ge(S["feat_done"], g + 1)
                if g >= 1:
                    te.wait_ge(S["ft_done"], g)
                for t in range(GT):
                    mm = te.transpose(pF[:, t * P:(t + 1) * P], featT[:, (g * GT + t) * P:(g * GT + t + 1) * P], ident[:, :])
                mm.then_inc(S["tf"], 1)

            def p_gt(g):
                b = g // GB
                te.wait_ge(S["ft_done"], g + 1)
                for t in range(GT):
                    mm = te.matmul(pGL[b][:, 0:P], xn[:, g % 4, t, :], feat[:, g * GT + t, :],
                                   start=(g % GB == 0 and t == 0), stop=(g % GB == GB - 1 and t == GT - 1))
                mm.then_inc(S["gt_done"], 1)

            def p_kv(b):
                te.wait_ge(S["gts_done"], b + 1)
                te.wait_ge(S["ks_done"], b + 1)
                te.wait_ge(S["prep_done"], 1)
                te.matmul(pH0[:, 0:P], wqm[:, b, :], gts[:, b, :], start=True, stop=False)
                te.matmul(pH0[:, 0:P], qbias[:, b, :], kdiag[:, b, :], start=False, stop=True).then_inc(S["kv_ready"], 1)
                te.wait_ge(S["kvt_done"], b + 1)
                if b:
                    te.wait_ge(S["mall_done"], b)
                te.matmul(pH1[:, 0:D + F], kvt[:, b, :], wmx[:, :], start=True, stop=True).then_inc(S["mall_ready"], 1)

            for s in range(G + 3):
                if s < G:
                    p_tx(s)
                if s == 0:
                    te.wait_ge(S["ld_attn"], 16 * 9)
                    for b in range(B):
                        te.matmul(pH[b][:, 0:512], siluB[:, b, :], wmod_sb[:, 0:512], start=True, stop=True)
                        mm = te.matmul(pQ[b][:, 0:256], siluB[:, b, :], wmod_sb[:, 512:768], start=True, stop=True)
                        mm.then_inc(S["mod_rows"], 1)
                    te.transpose(pF[:, 0:P], wm[:, :], ident[:, :]).then_inc(S["wmT_ready"], 1)
                    te.wait_ge(S["cols_ready"], 1)
                    for b in range(B):
                        mm = te.matmul(pL[:, b * P:(b + 1) * P], saB[:, b, :], wq[:, :], start=True, stop=True)
                    mm.then_inc(S["qb_ready"], 1)
                    te.wait_ge(S["wmT_done"], 1)
                    te.matmul(pF[:, 0:F], wmT[:, :], w1[:, :], start=True, stop=True).then_inc(S["wmw1_ready"], 1)
                    te.wait_ge(S["rows_read"], 2)
                    te.wait_ge(S["wmx_done"], 1)
                    te.wait_ge(S["cols_ready"], 1)
                if 0 <= s - 1 < G:
                    p_q(s - 1)
                if 0 <= s - 2 < G:
                    p_tf(s - 2)
                if 0 <= s - 3 < G:
                    if s - 3 == GB:
                        te.wait_ge(S["prep_done"], 1)
                    p_gt(s - 3)
                if s == GB + 3:
                    p_kv(0)
            p_kv(1)

            def p_den(g):
                b = g // GB
                if g >= 1:
                    te.wait_ge(S["z_done"], g)
                for t in range(GT):
                    mm = te.matmul(pG[:, t * H:(t + 1) * H], featT[:, (g * GT + t) * P:(g * GT + t + 1) * P],
                                   ksel[:, b, :], start=True, stop=True)
                mm.then_inc(S["den_ready"], 1)

            def p_tq(g):
                te.wait_ge(S["qp_done"], g + 1)
                if g >= 1:
                    te.wait_ge(S["qT_done"], g)
                for t in range(GT):
                    mm = te.transpose(pF[:, t * P:(t + 1) * P], qp[:, g % 2, t * P:(t + 1) * P], ident[:, :])
                mm.then_inc(S["tq"], 1)

            def p_y1(g):
                b = g // GB
                te.wait_ge(S["qT_done"], g + 1)
                if g % GB == 0:
                    te.wait_ge(S["mall_done"], b + 1)
                if g >= 1:
                    te.wait_ge(S["u1_done"], g)
                for t in range(GT):
                    mm = te.matmul(pQ0[:, t * D:(t + 1) * D], qT[:, g % 2, t * P:(t + 1) * P], mall[:, b, 0:D],
                                   start=True, stop=True)
                mm.then_inc(S["y1_ready"], 1)
                if g >= 1:
                    te.wait_ge(S["relu0"], g)
                    te.wait_ge(S["relu1"], g)
                for f in range(2):
                    mm = te.matmul(pH[f][:, :], mall[:, b, D + f * P:D + (f + 1) * P], qT[:, g % 2, :], start=True, stop=True)
                mm.then_inc(S["m1_ready"], 1)

            def p_y2(g):
                te.wait_ge(S["relu0"], g + 1)
                te.wait_ge(S["relu1"], g + 1)
                if g >= 1:
                    te.wait_ge(S["u2_done"], g)
                for t in range(GT):
                    for f in range(2):
                        mm = te.matmul(pQ1[:, t * D:(t + 1) * D], hid[:, g % 2, f, t * P:(t + 1) * P], w2[:, f, :],
                                       start=(f == 0), stop=(f == 1))
                mm.then_inc(S["y2_ready"], 1)

            def p_tx3(g):
                te.wait_ge(S["xn3"], g + 1)
                if g >= 1:
                    te.wait_ge(S["h2_done"], g)
                for t in range(GT):
                    mm = te.transpose(pT[:, t * P:(t + 1) * P], xn[:, g % 4, t, :], ident[:, :])
                mm.then_inc(S["tx3"], 1)

            def p_lg(g):
                te.wait_ge(S["h2_done"], g + 1)
                for t in range(GT):
                    k = g * GT + t
                    mm = te.matmul(pL[:, k * E:(k + 1) * E], h2T[:, k * P:(k + 1) * P], wg[:, :], start=True, stop=True)
                mm.then_inc(S["lg_ready"], 1)

            for s in range(G + 7):
                if s < G:
                    p_den(s)
                if 0 <= s - 1 < G:
                    p_tq(s - 1)
                if 0 <= s - 2 < G:
                    p_y1(s - 2)
                if 0 <= s - 3 < G:
                    p_y2(s - 3)
                if 0 <= s - 5 < G:
                    p_tx3(s - 5)
                if 0 <= s - 6 < G:
                    p_lg(s - 6)

            te.wait_ge(S["probs"], 1)
            for b in range(B):
                mm = te.transpose(pT[:, b * P:(b + 1) * P], pr[:, b, :, :].rearrange("p e t -> p (e t)"), ident[:, :])
            mm.then_inc(S["prt_ready"], 1)
            with te.Fori(0, HI_ROUNDS + LO_ROUNDS) as r:
                te.wait_ge(S["counts"], r + 1)
                te.matmul(pG[:, 0:3], same16[:, :], cnt[:, :], start=True, stop=True).then_inc(S["totals"], 1)
            te.wait_ge(S["diagT"], 1)
            te.matmul(pG[:, 0:P], ones[:, :], thd[:, :], start=True, stop=True).then_inc(S["thr_ready"], 1)
            te.wait_ge(S["gt_ready"], 1)
            te.matmul(pF[:, 0:B * P], onesb[:, :], gt_b[:, :, :, :].rearrange("p b e t -> p (b e t)"),
                      start=True, stop=True).then_inc(S["cgt_ready"], 1)
            te.wait_ge(S["rsum_ready"], 1)
            te.matmul(pL[:, 0:B * E], before[:, :], rsum[:, :, :].rearrange("p b e -> p (b e)"), start=True, stop=False,
                      skip_group_check=True)
            te.matmul(pL[:, E:2 * E], onesb[:, :], rsum[:, 0, :], start=False, stop=True,
                      skip_group_check=True).then_inc(S["base_ready"], 1)

            te.wait_ge(S["ld_moe"], 32)
            te.wait_ge(S["x1_done"], G)

            def p_up(g, e, k):
                for f in range(2):
                    te.matmul((pH if k == 0 else pQ)[f][:, :], ew1[:, e, f * P:(f + 1) * P],
                              h2T[:, bass.ds(g * W, W)], start=True, stop=True).then_inc(S["eh_ready"], 1)

            def p_down(e, k):
                for t in range(GT):
                    for f in range(2):
                        mm = te.matmul((pT if k == 0 else pF)[:, t * D:(t + 1) * D], eh[:, k, f, t * P:(t + 1) * P],
                                       ew2[:, e, f, :], start=(f == 0), stop=(f == 1))
                mm.then_inc(S["ey_ready"], 1)

            te.wait_ge(S["route_done"], 1)
            with te.Fori(0, G) as g:
                p_up(g, 0, 0)
                for e in range(E):
                    k = e % 2
                    if e + 1 < E:
                        p_up(g, e + 1, 1 - k)
                    te.wait_ge(S["eh_done"], g * (2 * E) + 2 * e + 2)
                    te.wait_ge(S["ey_free"], g * E + e + 1)
                    p_down(e, k)

        @block.vector
        def _(ve_):
            dve = ve_
            n = 0

            def link(ins):
                nonlocal n
                n += 1
                ins.then_inc(S["dve"], 1)
                dve.wait_ge(S["dve"], n)

            def stats(g, ready, ring):
                for t in range(GT):
                    last = dve.bn_stats(bn[:, ring, t, :], x_sb[:, g * GT + t, :])
                link(last)
                for t in range(GT):
                    last = dve.bn_aggr(mv[:, ring, t, :], bn[:, ring, t, :])
                return last.then_inc(S[ready], 1)

            def normalise(g, ring):
                for t in range(GT):
                    last = dve.tensor_scalar(xn[:, g % 4, t, :], x_sb[:, g * GT + t, :], mv[:, ring, t, 0:1],
                                             rs[:, ring, t:t + 1], ALU.subtract, ALU.mult)
                return last

            def v_stats1(g):
                dve.wait_ge(ld_x[g], 16)
                stats(g, "stats1", g % 2)

            def v_xn1(g):
                dve.wait_ge(S["rs1"], g + 1)
                if g >= 4:
                    dve.wait_ge(S["gt_done"], g - 3)
                    dve.wait_ge(S["acc_done"], g - 3)
                normalise(g, g % 2).then_inc(S["xn1"], 1)

            def v_feat(g):
                dve.wait_ge(S["exp_done"], g + 1)
                link(dve.tensor_scalar(ex[:, g % 2, :], ex[:, g % 2, :], 1.0, None, ALU.min))
                dve.scalar_tensor_tensor(featT[:, g * W:(g + 1) * W], pQ[g % 2][:, :], 0.0, ex[:, g % 2, :], ALU.max, ALU.add,
                                         accum_out=ksp[:, g:g + 1]).then_inc(S["feat_done"], 1)

            v_stats1(0)
            dve.wait_ge(S["consts"], 1)
            dve.wait_ge(S["silu_exp"], 1)
            link(dve.tensor_scalar(ec[:, :], ec[:, :], 1.0, None, ALU.add))
            link(dve.reciprocal(ec[:, :], ec[:, :]))
            dve.wait_ge(S["ld_mod"], 32)
            dve.tensor_tensor(siluT[:, :], cT[:, :], ec[:, :], ALU.mult).then_inc(S["silu_done"], 1)
            dve.wait_ge(S["silu_done"], 1)
            v_xn1(0)
            for b in range(B):
                last = dve.tensor_scalar(siluB[:, b, :], ones[:, :], siluT[:, b:b + 1], None, ALU.mult)
            last.then_inc(S["silu_done"], 1)
            dve.wait_ge(S["mod_cols"], 1)
            link(dve.tensor_copy(colm[:, :, :].rearrange("p j b -> p (j b)"), pG[:, 0:8]))
            dve.tensor_scalar(colm[:, 1, :], colm[:, 1, :], 1.0, None, ALU.add)
            link(dve.tensor_scalar(colm[:, 3, :], colm[:, 3, :], 1.0, None, ALU.add))
            dve.tensor_scalar(saB[:, 0, :], ones[:, :], colm[:, 0, 0:1], None, ALU.mult)
            dve.tensor_scalar(saB[:, 1, :], ones[:, :], colm[:, 0, 1:2], None, ALU.mult).then_inc(S["cols_ready"], 1)
            dve.wait_ge(S["cols_ready"], 1)
            v_stats1(1)
            dve.wait_ge(S["ld_attn"], 16 * 9)
            link(dve.tensor_tensor(bsum[:, :], rows[:, 1, :], rows[:, 3, :], ALU.add))
            dve.wait_ge(S["mod_rows"], 2)
            for b in range(B):
                def clamp(dst, v):
                    link(dve.tensor_scalar(sgn[:, :], v, 0.0, 2.0, ALU.is_ge, ALU.mult))
                    link(dve.scalar_tensor_tensor(dst, sgn[:, :], 1.0, v, ALU.subtract, ALU.mult))
                    link(dve.tensor_scalar(dst, dst, 0.25, None, ALU.max))
                    link(dve.scalar_tensor_tensor(dst, sgn[:, :], 1.0, dst, ALU.subtract, ALU.mult))
                clamp(gaR[:, b, :], pH[b][:, 2 * D:3 * D])
                clamp(gbR[:, b, :], pQ[b][:, D:2 * D])
                link(dve.tensor_tensor(rD[:, b, :], pH[b][:, 0:D], bsum[:, :], ALU.add))
                dve.tensor_tensor(rD[:, b, :], rD[:, b, :], gaR[:, b, :], ALU.mult)
                dve.scalar_tensor_tensor(rA[:, b, :], pH[b][:, D:2 * D], 1.0, gaR[:, b, :], ALU.add, ALU.mult)\
                   .then_inc(S["rows_read"], 1)
                dve.tensor_tensor(rB[:, b, :], rows[:, 0, :], gaR[:, b, :], ALU.mult)
                last = dve.tensor_tensor(rC[:, b, :], rows[:, 2, :], gaR[:, b, :], ALU.mult)
            last.then_inc(S["rows_done"], 1)
            dve.wait_ge(S["wmT_ready"], 1)
            dve.tensor_copy(wmT[:, :], pF[:, 0:P]).then_inc(S["wmT_done"], 1)
            dve.reduce_sum(rowm[:, 0:1], wm[:, :], AX.X)
            link(dve.reduce_sum(rowm[:, 1:3], w2[:, :, :], AX.X))
            link(dve.tensor_scalar(rowm[:, 0:3], rowm[:, 0:3], -1.0 / D, None, ALU.mult))
            dve.tensor_scalar(wmx[:, 0:D], wm[:, :], rowm[:, 0:1], None, ALU.add)
            for k in range(2):
                dve.tensor_scalar(w2[:, k, :], w2[:, k, :], rowm[:, 1 + k:2 + k], None, ALU.add)
            for b in range(B):
                dve.tensor_scalar(wqm[:, b, :], wq[:, :], colm[:, 1, b:b + 1], None, ALU.mult)
            dve.wait_ge(S["wmw1_ready"], 1)
            dve.tensor_copy(wmx[:, D:D + F], pF[:, 0:F]).then_inc(S["wmx_done"], 1)
            dve.wait_ge(S["qb_ready"], 1)
            dve.tensor_copy(qbias[:, :, :].rearrange("p b d -> p (b d)"), pL[:, 0:2 * P]).then_inc(S["prep_done"], 1)
            v_xn1(1)

            def v_ksum(b):
                dve.wait_ge(S["feat_done"], GB * (b + 1))
                link(dve.reduce_sum(ksum[:, b:b + 1], ksp[:, b * GB:(b + 1) * GB], AX.X))
                dve.tensor_scalar(ksel[:, b, :], same16[:, 0:P:HD], ksum[:, b:b + 1], None, ALU.mult)
                dve.tensor_scalar(kdiag[:, b, :], ident[:, :], ksum[:, b:b + 1], None, ALU.mult).then_inc(S["ks_done"], 1)

            def v_kvt(b):
                dve.wait_ge(S["kv_ready"], b + 1)
                dve.tensor_tensor(kvt[:, b, :], pH0[:, 0:P], same16[:, :], ALU.mult).then_inc(S["kvt_done"], 1)

            for s in range(G + 1):
                if 0 <= s - 1 < G:
                    v_feat(s - 1)
                if s + 2 < G:
                    v_stats1(s + 2)
                    v_xn1(s + 2)
                if s == GB + 1:
                    v_ksum(0)
                if s == GB + 3:
                    v_kvt(0)
            v_ksum(1)
            v_kvt(1)

            def v_z(g):
                dve.wait_ge(S["den_ready"], g + 1)
                if g >= 2:
                    dve.wait_ge(S["qp_done"], g - 1)
                link(dve.tensor_scalar(z[:, g % 2, :], pG[:, 0:GT * H], ATTN_EPS, None, ALU.add))
                dve.reciprocal(z[:, g % 2, :], z[:, g % 2, :]).then_inc(S["z_done"], 1)

            def v_relu(g):
                dve.wait_ge(S["m1_ready"], g + 1)
                if g >= 2:
                    dve.wait_ge(S["y2_ready"], g - 1)
                dve.tensor_scalar(hid[:, g % 2, 1, :], pH1[:, :], 0.0, None, ALU.max).then_inc(S["relu1"], 1)

            def v_u1(g):
                dve.wait_ge(S["sq1"], g + 1)
                dve.tensor_tensor(u1[:, g % 2], pQ0[:, :].rearrange("p (t d) -> p t d", d=D), row4(rB[:, g // GB, :]),
                                  ALU.mult).then_inc(S["u1_done"], 1)

            def v_x1(g):
                dve.wait_ge(S["sq2"], g + 1)
                dve.tensor_tensor(u2[:, :, :], pQ1[:, :].rearrange("p (t d) -> p t d", d=D), row4(rC[:, g // GB, :]),
                                  ALU.mult).then_inc(S["u2_done"], 1)
                dve.wait_ge(S["yr_done"], g + 1)
                dve.wait_ge(S["u1_done"], g + 1)
                dve.wait_ge(S["acc_done"], g + 1)
                for t in range(GT):
                    xt = x_sb[:, g * GT + t, :]
                    last = dve.scalar_tensor_tensor(xt, u1[:, g % 2, t, :], yr[:, g % 2, t:t + 1], xt, ALU.mult, ALU.add)
                link(last)
                dve.wait_ge(S["u2_done"], g + 1)
                for t in range(GT):
                    xt = x_sb[:, g * GT + t, :]
                    last = dve.scalar_tensor_tensor(xt, u2[:, t, :], yr[:, g % 2, GT + t:GT + t + 1], xt, ALU.mult, ALU.add)
                last.then_inc(S["x1_done"], 1)
                dve.wait_ge(S["x1_done"], g + 1)
                stats(g, "stats3", g % 2)

            def v_xn3(g):
                dve.wait_ge(S["rs3"], g + 1)
                if g >= 4:
                    dve.wait_ge(S["tx3"], g - 3)
                else:
                    dve.wait_ge(S["gt_done"], G)
                normalise(g, g % 2).then_inc(S["xn3"], 1)

            for s in range(G + 5):
                if s < G:
                    v_z(s)
                if 0 <= s - 2 < G:
                    v_relu(s - 2)
                    v_u1(s - 2)
                if 0 <= s - 3 < G:
                    v_x1(s - 3)
                if 0 <= s - 4 < G:
                    v_xn3(s - 4)

            def flat(t):
                return t[:, :, :, :].rearrange("p b e t -> p (b e t)")

            def over_e(t, op, src):
                return dve.tensor_reduce(t, src.rearrange("p b e t -> p b t e"), AX.X, op)

            def b_et(t):
                return t[:, :, :].unsqueeze(2).to_broadcast([P, B, E, TB])

            def be_(t):
                return t[:, :, :].unsqueeze(3).to_broadcast([P, B, E, TB])

            def mul(o, a, b):
                return dve.tensor_tensor(o, a, b, ALU.mult)

            dve.wait_ge(S["lg_ready"], G)
            lg = pL[:, 0:NT * E].rearrange("p (b t e) -> p b e t", b=B, e=E)
            link(over_e(mx[:, :, :], ALU.max, lg))
            for b in range(B):
                last = dve.tensor_tensor(m1[:, b], lg[:, b], mx[:, b, :].unsqueeze(1).to_broadcast([P, E, TB]), ALU.subtract)
            last.then_inc(S["lmax"], 1)
            dve.wait_ge(S["exp2"], 1)
            link(over_e(sm[:, :, :], ALU.add, pe_[:, :, :, :]))
            link(dve.reciprocal(sm[:, :, :], sm[:, :, :]))
            for b in range(B):
                last = dve.tensor_tensor(pr[:, b], pe_[:, b], sm[:, b, :].unsqueeze(1).to_broadcast([P, E, TB]), ALU.mult)
            last.then_inc(S["probs"], 1)
            dve.wait_ge(S["prt_ready"], 1)
            link(dve.tensor_copy(prT[:, :], pT[:, 0:B * P]))
            bits = prT[:, :].bitcast(I32)
            link(dve.tensor_scalar(ki[:, :], bits, HI_SHIFT, None, ALU.logical_shift_right))
            link(dve.tensor_copy(khi[:, :], ki[:, :]))
            link(dve.tensor_scalar(ki[:, :], bits, (1 << HI_SHIFT) - 1, None, ALU.bitwise_and))
            link(dve.tensor_copy(klo[:, :], ki[:, :]))

            def search(keys, col0, rounds, done0, k):
                link(dve.tensor_scalar(cur[:, k, :], jc[:, :], steps[:, col0:col0 + 1], None, ALU.mult))
                with dve.Fori(0, rounds) as r:
                    for j in range(3):
                        last = dve.tensor_scalar(junk[:, j, :], keys, cur[:, k, j + 1:j + 2], None, ALU.is_ge, ALU.add,
                                                 accum_out=cnt[:, j:j + 1])
                    last.then_inc(S["counts"], 1)
                    dve.scalar_tensor_tensor(pre[:, :], jc[:, :], steps[:, bass.ds(r + (col0 + 1), 1)],
                                             cur[:, k, 0:1].to_broadcast([P, 4]), ALU.mult, ALU.add)
                    dve.wait_ge(S["totals"], r + (done0 + 1))
                    dve.tensor_scalar(dig[:, :], pG[:, 0:3], CAP - 0.5, None, ALU.is_ge, ALU.add,
                                      accum_out=digit[:, :]).then_inc(S["digits"], 1)
                    dve.wait_ge(S["digits"], r * 2 + (2 * done0 + 1))
                    dve.scalar_tensor_tensor(cur[:, k, :], digit[:, 0:1].to_broadcast([P, 4]),
                                             steps[:, bass.ds(r + col0, 1)], pre[:, :], ALU.mult, ALU.add).then_inc(S["digits"], 1)
                    dve.wait_ge(S["digits"], r * 2 + (2 * done0 + 2))

            search(khi[:, :], 8 - HI_ROUNDS, HI_ROUNDS, 0, 0)
            link(dve.tensor_scalar(khi[:, :], khi[:, :], cur[:, 0, 0:1], 65536.0, ALU.subtract, ALU.mult))
            link(dve.tensor_tensor(klo[:, :], khi[:, :], klo[:, :], ALU.add))
            search(klo[:, :], 8 - LO_ROUNDS, LO_ROUNDS, HI_ROUNDS, 1)
            link(dve.tensor_copy(thi[:, :], cur[:, :, 0]))
            link(dve.tensor_scalar(thi[:, 0:1], thi[:, 0:1], HI_SHIFT, None, ALU.logical_shift_left))
            link(dve.tensor_tensor(thi[:, 0:1], thi[:, 0:1], thi[:, 1:2], ALU.bitwise_or))
            dve.tensor_scalar(thd[:, :], ident[:, :], thi[:, 0:1].bitcast(F32), None, ALU.mult).then_inc(S["diagT"], 1)
            dve.wait_ge(S["thr_ready"], 1)
            link(dve.tensor_copy(thr[:, :], pG[:, 0:P]))
            tb = thr[:, :].unsqueeze(1).to_broadcast([P, B, P])
            pf = pr[:, :, :, :].rearrange("p b e t -> p b (e t)")
            dve.tensor_tensor(gt_b[:, :, :, :].rearrange("p b e t -> p b (e t)"), pf, tb, ALU.is_gt).then_inc(S["gt_ready"], 1)
            link(dve.tensor_tensor(eq[:, :, :, :].rearrange("p b e t -> p b (e t)"), pf, tb, ALU.is_equal))
            link(dve.tensor_tensor_scan(flat(scan), segmask[:, :], flat(eq), 0.0, ALU.mult, ALU.add))
            dve.tensor_copy(rsum[:, :, :], scan[:, :, :, TB - 1]).then_inc(S["rsum_ready"], 1)
            dve.wait_ge(S["rsum_ready"], 1)
            link(dve.tensor_tensor(flat(scan), flat(scan), flat(eq), ALU.subtract))
            dve.wait_ge(S["cgt_ready"], 1)
            link(dve.tensor_reduce(base[:, :, :], pF[:, 0:B * P].rearrange("p (b e t) -> p b e t", b=B, e=E), AX.X, ALU.add))
            link(dve.tensor_tensor(cgt[:, :], base[:, 0, :], base[:, 1, :], ALU.add))
            dve.wait_ge(S["base_ready"], 1)
            link(dve.tensor_tensor(base[:, :, :], pL[:, 0:B * E].rearrange("p (b e) -> p b e", b=B),
                                   cgt[:, :].unsqueeze(1).to_broadcast([P, B, E]), ALU.add))
            for b in range(B):
                last = dve.tensor_tensor(m1[:, b], scan[:, b], base[:, b, :].unsqueeze(2).to_broadcast([P, E, TB]), ALU.add)
            link(last)
            link(dve.scalar_tensor_tensor(flat(m2), flat(m1), CAP - 0.5, flat(eq), ALU.is_lt, ALU.mult))
            link(dve.tensor_tensor(flat(sel), flat(m2), flat(gt_b), ALU.add))
            link(over_e(anys[:, :, :], ALU.max, sel[:, :, :, :]))
            for b in range(B):
                last = dve.scalar_tensor_tensor(m1[:, b], sel[:, b], 1.0, anys[:, b, :].unsqueeze(1).to_broadcast([P, E, TB]),
                                                ALU.subtract, ALU.mult)
            link(last)
            link(dve.scalar_tensor_tensor(flat(m1), flat(m1), 2.0, flat(pr), ALU.mult, ALU.add))
            link(over_e(mx[:, :, :], ALU.max, m1[:, :, :, :]))
            for b in range(B):
                last = dve.tensor_tensor(m2[:, b], m1[:, b], mx[:, b, :].unsqueeze(1).to_broadcast([P, E, TB]), ALU.is_ge)
            link(last)
            link(dve.tensor_scalar(flat(m2), flat(m2), -8.0, 8.0, ALU.mult, ALU.add))
            for b in range(B):
                last = dve.tensor_tensor(m2[:, b], m2[:, b], eidx[:, :].unsqueeze(2).to_broadcast([P, E, TB]), ALU.add)
            link(last)
            link(over_e(sm[:, :, :], ALU.min, m2[:, :, :, :]))
            for b in range(B):
                last = dve.tensor_tensor(m1[:, b], m2[:, b], sm[:, b, :].unsqueeze(1).to_broadcast([P, E, TB]), ALU.is_equal)
            link(last)
            for b in range(B):
                last = dve.tensor_tensor(gate[:, b * TB:(b + 1) * TB, :].rearrange("p t e -> p e t"), m1[:, b],
                                         mx[:, b, :].unsqueeze(1).to_broadcast([P, E, TB]), ALU.mult)
            last.then_inc(S["route_done"], 1)
            dve.wait_ge(S["route_done"], 1)

            dve.memset(digit[:, :], 0.0).then_inc(S["ey_free"], 1)
            dve.memset(dig[:, :], 0.0).then_inc(S["ey_free"], 1)
            with dve.Fori(0, B) as b:
                with dve.Fori(0, GB) as q:
                    for e in range(E):
                        bank = (pT, pF)[e % 2]
                        dve.wait_ge(S["ey_ready"], b * (GB * E) + q * E + e + 1)
                        for t in range(GT):
                            gs = gate[:, bass.ds(b * TB + q * GT + t, 1), e]
                            yt = bank[:, t * D:(t + 1) * D]
                            if e == 0:
                                last = dve.tensor_scalar(ya[:, t, :], yt, gs, None, ALU.mult)
                            else:
                                last = dve.scalar_tensor_tensor(ya[:, t, :], yt, gs, ya[:, t, :], ALU.mult, ALU.add)
                        last.then_inc(S["ey_free"], 1)
                        dve.wait_ge(S["ey_free"], b * (GB * E) + q * E + e + 3)
                    dve.tensor_tensor(ya[:, :, :], ya[:, :, :], gbR[:, bass.ds(b, 1), :].to_broadcast([P, GT, D]), ALU.mult)\
                       .then_inc(S["gated"], 1)
                    dve.wait_ge(S["gated"], b * GB + q + 1)
                    xt = x_sb[:, bass.ds(b * TB + q * GT, GT), :]
                    dve.tensor_tensor(xt, xt, ya[:, :, :], ALU.add).then_inc(S["o_done"], 1)
                    dve.wait_ge(S["o_done"], b * GB + q + 1)


_INS = ['L0_attn_x', 'L0_attn_Wq', 'L0_attn_Wm', 'L0_attn_W1', 'L0_attn_W2', 'L0_attn_g1', 'L0_attn_b1', 'L0_attn_g2',
        'L0_attn_b2', 'L0_ffn_Wg', 'L0_ffn_W1', 'L0_ffn_W2', 'L0_c', 'L0_wmod']


def kernel(**inputs):
    import numpy as _np
    import concourse.bacc as _bacc
    from concourse import mybir as _mybir
    from concourse.bass_utils import run_bass_kernel_spmd as _run

    nc = _bacc.Bacc("TRN2", target_bir_lowering=False, num_devices=1)
    arrays, args = {}, []
    for name in _INS:
        a = _np.ascontiguousarray(inputs[name])
        arrays[f"in_{name}_dram"] = a
        args.append(nc.dram_tensor(f"in_{name}_dram", a.shape, _mybir.dt.from_np(a.dtype), kind="ExternalInput").ap())
    out = nc.dram_tensor("out_dram", (B, L, D), F32, kind="ExternalOutput").ap()
    build(nc, *args, out)
    r = _run(nc, [arrays], core_ids=[0])
    return r.results[0]["out_dram"]
```

```python
from contextlib import ExitStack

import concourse.bass as bass
from concourse import mybir

F32 = mybir.dt.float32
BF16 = mybir.dt.bfloat16
I32 = mybir.dt.int32
ALU = mybir.AluOpType
ACT = mybir.ActivationFunctionType
AX = mybir.AxisListType

P = 128
B, L, D = 2, 2048, 128
H, HD = 8, 16
E, F = 8, 256
CAP = B * L // E
TB = L // P
NT = B * TB
GT = 4
G = NT // GT
GB = G // B
W = GT * P
LN_EPS = 1e-5
ATTN_EPS = 1e-6
BITS = 3
HALF = 15
ROUNDS = HALF // BITS
NC = 2 ** BITS
DV = 5
MT = NT + E - 1
NJ = MT
R = 8
RW = 4
POOLQ = 3
NL = NJ // R * R


def build(nc, x, Wq, Wm, W1, W2, g1, b1, g2, b2, Wg, EW1, EW2, c, wmod, table, out):
    with ExitStack() as ctx:
        def sb(name, shape, dt=F32):
            return ctx.enter_context(nc.sbuf_tensor(name, shape, dt))

        def psum(name):
            return ctx.enter_context(nc.psum_tensor(name, [P, 512], F32))

        def sem(name):
            return ctx.enter_context(nc.semaphore(name))

        x_sb = sb("x_sb", [P, NT, D])
        featT = sb("featT", [P, NT * P])
        feat = sb("feat", [P, NT, D])
        h2 = sb("h2", [P, NT, D])
        ew = sb("ew", [P, E, 2 * F])

        wq = sb("wq", [P, D]); wm = sb("wm", [P, D]); w1 = sb("w1", [P, F]); w2 = sb("w2", [P, 2, D])
        wg = sb("wg", [P, E]); wmod_sb = sb("wmod_sb", [P, 6 * D]); cT = sb("cT", [P, B])
        rows = sb("rows", [P, 4, D])
        wmT = sb("wmT", [P, D])
        wmx = sb("wmx", [P, D + F])
        wqm = sb("wqm", [P, B, D])
        qbias = sb("qbias", [P, B, D])

        ident = sb("ident", [P, P]); ones = sb("ones", [P, P]); same16 = sb("same16", [P, P])
        before = sb("before", [P, P], BF16); onesb = sb("onesb", [P, P], BF16)
        neghalf = sb("neghalf", [P, 8]); steps = sb("steps", [P, ROUNDS + 1]); jc = sb("jc", [P, NC])
        half16 = sb("half16", [P, P]); c16 = sb("c16", [P, NC - DV]); iota = sb("iota", [P, P], BF16)
        iotaj = sb("iotaj", [P, NJ + 2])
        eidx = sb("eidx", [P, E]); segmask = sb("segmask", [P, NT * E])

        ec = sb("ec", [P, B]); siluT = sb("siluT", [P, B]); siluB = sb("siluB", [P, B, P])
        colm = sb("colm", [P, 4, B])
        saB = sb("saB", [P, B, P])
        gaR = sb("gaR", [P, B, D]); gbR = sb("gbR", [P, B, D]); sgn = sb("sgn", [P, B, D]); modr = sb("modr", [P, B, 5 * D])
        rA = sb("rA", [P, B, D]); rB = sb("rB", [P, B, D]); rC = sb("rC", [P, B, D]); rD = sb("rD", [P, B, D])
        cbR = sb("cbR", [P, B, D]); sbR = sb("sbR", [P, B, D]); dgb = sb("dgb", [P, D])
        bsum = sb("bsum", [P, D]); rowm = sb("rowm", [P, 4])

        bn = sb("bn", [P, G, GT, 6]); mv = sb("mv", [P, G, GT, 2]); ve = sb("ve", [P, G, GT]); rs = sb("rs", [P, G, GT])
        xn = sb("xn", [P, G, GT, D]); h2T = sb("h2T", [P, 2, W]); hT = sb("hT", [P, 2, W]); ex = sb("ex", [P, 2, W])
        ksp = sb("ksp", [P, G]); ksum = sb("ksum", [P, B]); ksel = sb("ksel", [P, B, H]); kdiag = sb("kdiag", [P, B, P])
        gts = sb("gts", [P, B, P]); kvt = sb("kvt", [P, B, P]); mall = sb("mall", [P, B, D + F])
        z = sb("z", [P, 2, GT * H]); qp = sb("qp", [P, 2, W]); qT = sb("qT", [P, 2, W])
        hid = sb("hid", [P, 2, 2, W]); ssq = sb("ssq", [P, 2, 2 * GT]); yv = sb("yv", [P, 2, 2 * GT]); yr = sb("yr", [P, 2, 2 * GT])
        u1 = sb("u1", [P, 3, GT, D]); u2 = sb("u2", [P, 2, GT, D]); t2 = sb("t2", [P, GT, D]); t1 = sb("t1", [P, GT, D]); sqj = sb("sqj", [P, 2, 2 * GT, D], BF16)

        mx = sb("mx", [P, B, TB]); pr = sb("pr", [P, B, E, TB]); pe_ = sb("pe_", [P, B, E, TB]); sm = sb("sm", [P, B, TB])
        prT = sb("prT", [P, B * P]); khi = sb("khi", [P, B * P]); ki = sb("ki", [P, B * P], I32); klo = sb("klo", [P, B * P])
        cur = sb("cur", [P, 2, NC]); pre = sb("pre", [P, NC]); cnt = sb("cnt", [P, NC]); dig = sb("dig", [P, NC - 1])
        ncur = sb("ncur", [P, NC - DV])
        digit = sb("digit", [P, 1]); thi = sb("thi", [P, 2], I32); thd = sb("thd", [P, P]); thr = sb("thr", [P, P])
        gt_b = sb("gt_b", [P, B, E, TB], BF16); eq = sb("eq", [P, B, E, TB]); scan = sb("scan", [P, B, E, TB])
        rsum = sb("rsum", [P, B, E], BF16); base = sb("base", [P, B, E]); cgt = sb("cgt", [P, E])
        sel = sb("sel", [P, B, E, TB]); m1 = sb("m1", [P, B, E, TB]); m2 = sb("m2", [P, B, E, TB]); anys = sb("anys", [P, B, TB])
        tot = sb("tot", [P, E]); toti = sb("toti", [P, E], I32); ntile = sb("ntile", [P, E]); tend = sb("tend", [P, E])
        posi = sb("posi", [P, NT], I32); loi = sb("loi", [P, NT], I32); hii = sb("hii", [P, NT], I32)
        lo = sb("lo", [P, NT]); hi = sb("hi", [P, NT])
        val = sb("val", [P, 5, NT], BF16)
        inv = sb("inv", [P, 5, NJ]); idf = sb("idf", [P, NJ]); oob = sb("oob", [P, NJ])
        gidx = sb("gidx", [P, NJ], I32)
        sidx = sb("sidx", [P, NJ], I32)
        flag = sb("flag", [P, NJ]); wslot = sb("wslot", [P, NJ])
        eidf = sb("eidf", [P, NJ + 2]); eid = sb("eid", [P, NJ + 2], I32)

        spaces = {"featT": featT[:, :], "feat": feat[:, :, :].rearrange("p t d -> p (t d)"),
                  "xn": xn[:, :, :, :].rearrange("p g t d -> p (g t d)")}
        used = dict.fromkeys(spaces, 0)

        def take(name, width):
            at = used[name]
            used[name] = at + width
            return spaces[name][:, at:at + width]

        def bf16(words, width, *dims):
            v = words.bitcast(BF16)
            return v.rearrange("p (t c) -> p t c", c=width) if not dims else v.rearrange("p (t v c) -> p t v c", v=dims[0], c=width)

        ohlo = bf16(take("featT", NT * P // 2), P)
        ohhi = bf16(take("feat", NT * NJ // 2), NJ)
        ohi = bf16(take("feat", NT * 2 * NJ // 2), NJ, 2)
        ohw = bf16(take("featT", NT * 3 * NJ // 2), NJ, 3)
        ecmp = take("feat", (NJ + 2) * E).rearrange("p (j e) -> p j e", e=E)
        row = take("xn", R * 2 * D).rearrange("p (k c) -> p k c", c=2 * D)
        o_sb = take("xn", R * D).rearrange("p (k c) -> p k c", c=D)
        junk = take("xn", NC * B * P // 2).bitcast(BF16).rearrange("p (n c) -> p n c", c=B * P)
        wcur = hid[:, :, :, :].rearrange("p a f c -> p (a f) c")
        eh = u2[:, 0, :, :].rearrange("p (k a) d -> p k (a d)", k=2)
        xt = u2[:, 1, 0:2, :]
        gsel, yw = u1[:, 0], u1[:, 1]

        pT, pF, pQ0, pQ1, pH0, pH1, pG, pL = (psum(n) for n in ("pT", "pF", "pQ0", "pQ1", "pH0", "pH1", "pG", "pL"))
        pQ, pH, pGL = (pQ0, pQ1), (pH0, pH1), (pG, pL)

        names = """ld_mod ld_attn ld_moe consts
            silu_exp silu_done mod_cols cols_ready mod_rows rows_read wmT_ready wmT_done wmw1_ready wmx_done qb_ready prep_done rows_done
            stats1 rs1 xn1 tx hT_done q_ready exp_done feat_done tf ft_done gt_done acc_done
            ks_done gts_done kv_ready kvt_done mall_ready mall_done
            den_ready z_done qp_done tq qT_done y1_ready m1_ready relu0 relu1 y2_ready sq1 sq2 u1_done u2_done yr_done x1_done
            stats3 rs3 xn3 tx3 h2_done lg_ready
            lmax exp2 probs prt_ready counts totals keys diagT thr_ready gt_ready cgt_ready rsum_ready base_ready route_done
            tab_done h2t_done acounts ncur_ready
            rank_ready rbase_ready slot_ready lo_ready hi_ready inv_ready ohw_ready slots_done
            w_done xt_ready xt_done up_ready eh_done y_ready y_free gsel_done o_done digits dve pool""".split()
        S = {n: sem(n) for n in names}
        ld_x = [sem(f"ld_x{g}") for g in range(G)]
        gathered = [sem(f"gathered{k}") for k in range(R)]
        scattered = [sem(f"scattered{k}") for k in range(R)]

        block = ctx.enter_context(nc.Block())

        def bgroup(t, g):
            return t[:, g * GT:(g + 1) * GT, :]

        def row4(r):
            return r.unsqueeze(1).to_broadcast([P, GT, D])

        @block.sync
        def _(sp):
            xv = x.rearrange("b (p t) d -> b p t d", p=P)
            tv = table.rearrange("(b p t) c -> b p t c", b=B, p=P)
            sp.dma_start(bgroup(x_sb, 0), xv[0, :, 0:GT, :]).then_inc(ld_x[0], 16)
            sp.dma_start(wmod_sb[:, :], wmod).then_inc(S["ld_mod"], 16)
            for g in range(1, G):
                t0 = g % GB * GT
                sp.dma_start(bgroup(x_sb, g), xv[g // GB, :, t0:t0 + GT, :]).then_inc(ld_x[g], 16)
            sp.dma_start(ew[:, :, 0:F], EW1.rearrange("e d f -> d e f")).then_inc(S["ld_moe"], 16)
            for k in range(2):
                sp.dma_start(ew[:, :, F + k * D:F + (k + 1) * D], EW2.rearrange("e (k p) d -> k p e d", p=P)[k]).then_inc(S["ld_moe"], 16)
            for g in range(G):
                t0 = g % GB * GT
                sp.wait_ge(S["x1_done"], g + 1)
                sp.dma_start(tv[g // GB, :, t0:t0 + GT, D:2 * D], bgroup(x_sb, g)).then_inc(S["tab_done"], 16)
                sp.wait_ge(S["h2t_done"], g + 1)
                sp.dma_start(tv[g // GB, :, t0:t0 + GT, 0:D], bgroup(h2, g)).then_inc(S["tab_done"], 16)
            for k in range(R):
                sp.wait_ge(scattered[k], 16 * ((NJ - 1 - k) // R + 1))

        @block.gpsimd
        def _(gp):
            n = 0

            def link(ins):
                nonlocal n
                n += 1
                ins.then_inc(S["pool"], 1)
                gp.wait_ge(S["pool"], n)

            gp.memset(ident[:, :], 0.0)
            gp.memset(ones[:, :], 1.0)
            gp.memset(onesb[:, :], 1.0)
            gp.memset(same16[:, :], 1.0)
            gp.memset(before[:, :], 1.0)
            gp.memset(neghalf[:, :], -0.5)
            gp.memset(segmask[:, :], 1.0)
            gp.memset(half16[:, :], 0.5)
            gp.memset(c16[:, :], float(NT // 2))
            for k in range(ROUNDS + 1):
                gp.memset(steps[:, k:k + 1], float(NC) ** (ROUNDS - 1 - k))
            for k in range(NC):
                gp.memset(jc[:, k:k + 1], float(k))
            link(gp.memset(rowm[:, 0:1], 0.0))
            gp.affine_select(out=ident[:, :], in_=ident[:, :], compare_op=ALU.not_equal, fill=1.0, base=0,
                             pattern=[[-1, P]], channel_multiplier=1)
            gp.affine_select(out=before[:, :], in_=before[:, :], compare_op=ALU.is_gt, fill=0.0, base=0,
                             pattern=[[1, P]], channel_multiplier=-1)
            gp.affine_select(out=segmask[:, :], in_=segmask[:, :], compare_op=ALU.not_equal, fill=0.0, base=0,
                             pattern=[[0, B * E], [1, TB]], channel_multiplier=0)
            gp.iota(eidx[:, :], pattern=[[1, E]], base=0, channel_multiplier=0, allow_small_or_imprecise_dtypes=True)
            gp.iota(iota[:, :], pattern=[[1, P]], base=0, channel_multiplier=0, allow_small_or_imprecise_dtypes=True)
            gp.iota(iotaj[:, :], pattern=[[1, NJ + 2]], base=0, channel_multiplier=0, allow_small_or_imprecise_dtypes=True)
            for b in range(B):
                gp.iota(val[:, 0, b * TB:(b + 1) * TB], pattern=[[0, TB]], base=b * L, channel_multiplier=TB,
                        allow_small_or_imprecise_dtypes=True)
                gp.iota(val[:, 1, b * TB:(b + 1) * TB], pattern=[[1, TB]], base=1, channel_multiplier=0,
                        allow_small_or_imprecise_dtypes=True)
            for m in (half16, same16):
                blocks = m[:, :].rearrange("p (h c) -> p h c", c=HD)
                link(gp.affine_select(out=blocks, in_=blocks, compare_op=ALU.is_ge, fill=0.0, base=0,
                                      pattern=[[-HD, H], [0, HD]], channel_multiplier=1))
                last = gp.affine_select(out=blocks, in_=blocks, compare_op=ALU.is_ge, fill=0.0, base=HD - 1,
                                        pattern=[[HD, H], [0, HD]], channel_multiplier=-1)
            last.then_inc(S["consts"], 1)

            def rsqrt(dst, src, tmp, scale, eps, width):
                link(gp.tensor_scalar(tmp, src, scale, eps, ALU.mult, ALU.add))
                return gp.tensor_tensor(dst, tmp, neghalf[:, 0:width], ALU.pow)

            def rs_a(g):
                gp.wait_ge(S["stats1"], g + 1)
                rsqrt(rs[:, g, :], mv[:, g, :, 1], ve[:, g, :], 1.0, LN_EPS, GT).then_inc(S["rs1"], 1)

            def acc(g):
                b = g // GB
                gp.wait_ge(S["xn1"], g + 1)
                if g:
                    gp.wait_ge(S["acc_done"], g)
                link(gp.tensor_tensor(t1[:, :, :], xn[:, g], row4(rA[:, b, :]), ALU.mult))
                link(gp.tensor_tensor(t1[:, :, :], t1[:, :, :], row4(rD[:, b, :]), ALU.add))
                gp.tensor_tensor(bgroup(x_sb, g), bgroup(x_sb, g), t1[:, :, :], ALU.add).then_inc(S["acc_done"], 1)

            rs_a(0)
            rs_a(1)
            rs_a(2)
            for g in range(G):
                if g + 3 < G:
                    rs_a(g + 3)
                if g == 0:
                    gp.wait_ge(S["rows_done"], 1)
                acc(g)

            def qprime(g):
                gp.wait_ge(S["z_done"], g + 1)
                if g >= 2:
                    gp.wait_ge(S["tq"], g - 1)
                gp.wait_ge(S["ft_done"], g + 1)
                gp.tensor_tensor(qp[:, g % 2, :].rearrange("p (t c) -> p t c", c=HD),
                                 bgroup(feat, g).rearrange("p t (h c) -> p (t h) c", c=HD),
                                 z[:, g % 2, :].unsqueeze(2).to_broadcast([P, GT * H, HD]), ALU.mult).then_inc(S["qp_done"], 1)

            def yrs(g):
                gp.wait_ge(S["sq1"], g + 1)
                gp.wait_ge(S["sq2"], g + 1)
                if g >= 2:
                    gp.wait_ge(S["x1_done"], g - 1)
                rsqrt(yr[:, g % 2, :], ssq[:, g % 2, :], yv[:, g % 2, :], 1.0 / D, LN_EPS, 2 * GT).then_inc(S["yr_done"], 1)

            def rs3(g):
                gp.wait_ge(S["stats3"], g + 1)
                rsqrt(rs[:, g, :], mv[:, g, :, 1], ve[:, g, :], 1.0, LN_EPS, GT).then_inc(S["rs3"], 1)

            def h2tok(g):
                gp.wait_ge(S["xn3"], g + 1)
                if g:
                    gp.wait_ge(S["h2t_done"], g)
                link(gp.tensor_tensor(t2[:, :, :], xn[:, g], row4(cbR[:, g // GB, :]), ALU.mult))
                gp.tensor_tensor(bgroup(h2, g), t2[:, :, :], row4(sbR[:, g // GB, :]), ALU.add).then_inc(S["h2t_done"], 1)

            for s in range(G + 6):
                if s < G:
                    qprime(s)
                if 0 <= s - 5 < G:
                    h2tok(s - 5)
                if 0 <= s - 4 < G:
                    rs3(s - 4)
                if 0 <= s - 3 < G:
                    yrs(s - 3)

            gp.wait_ge(S["slot_ready"], 1)
            nq = NT // 4
            for q in range(POOLQ, 4):
                for t in range(q * nq, (q + 1) * nq):
                    last = gp.tensor_scalar(ohlo[:, t, :], iota[:, :], lo[:, t:t + 1], None, ALU.is_equal)
                last.then_inc(S["lo_ready"], 1)
            gp.wait_ge(S["slots_done"], 1)
            gp.wait_ge(S["tab_done"], 16 * 2 * G)

            def gather(j):
                gp.indirect_dma_start(row[:, j % R, :], None, table[:, :], bass.IndirectOffsetOnAxis(gidx[:, j:j + 1], 0),
                                      bounds_check=B * L - 1, oob_is_err=False).then_inc(gathered[j % R], 16)

            def scatter(j):
                gp.indirect_dma_start(out.rearrange("b l d -> (b l) d"), bass.IndirectOffsetOnAxis(sidx[:, j:j + 1], 0),
                                      o_sb[:, j % R, :], None, bounds_check=B * L - 1, oob_is_err=False).then_inc(scattered[j % R], 16)

            for k in range(R):
                gather(k)
            for j in range(NJ):
                gp.wait_ge(S["o_done"], j + 1)
                scatter(j)
                if j + R < NJ:
                    gather(j + R)

        @block.scalar
        def _(act):
            n = 0
            act.dma_start(cT[:, :], c.rearrange("b d -> d b"), allow_slow_non_contiguous=True).then_inc(S["ld_mod"], 16)
            for dst, src in ((wq[:, :], Wq), (wm[:, :], Wm), (w1[:, :], W1), (w2[:, :, :], W2.rearrange("(k p) d -> p k d", p=P)),
                             (wg[:, :], Wg)):
                act.dma_start(dst, src).then_inc(S["ld_attn"], 16)
            for n, r in enumerate((g1, b1, g2, b2)):
                act.dma_start(rows[:, n, :], r.partition_broadcast(P)).then_inc(S["ld_attn"], 16)
            act.wait_ge(S["ld_mod"], 32)
            act.activation(ec[:, :], cT[:, :], ACT.Exp, scale=-1.0).then_inc(S["silu_exp"], 1)
            act.wait_ge(S["cols_ready"], 1)

            def a_hT(g):
                b = g // GB
                act.wait_ge(S["tx"], g + 1)
                if g >= 2:
                    act.wait_ge(S["q_ready"], g - 1)
                act.activation(hT[:, g % 2, :], pT[:, :], ACT.Identity, bias=colm[:, 0, b:b + 1],
                               scale=colm[:, 1, b:b + 1]).then_inc(S["hT_done"], 1)

            def a_exp(g):
                act.wait_ge(S["q_ready"], g + 1)
                if g >= 2:
                    act.wait_ge(S["feat_done"], g - 1)
                act.activation(ex[:, g % 2, :], pQ[g % 2][:, :], ACT.Exp).then_inc(S["exp_done"], 1)

            def a_ft(g):
                act.wait_ge(S["tf"], g + 1)
                act.copy(bgroup(feat, g), pF[:, :].rearrange("p (t d) -> p t d", d=D)).then_inc(S["ft_done"], 1)

            def a_kv(b):
                act.wait_ge(S["gt_done"], GB * (b + 1))
                act.copy(gts[:, b, :], pGL[b][:, 0:P]).then_inc(S["gts_done"], 1)
                act.wait_ge(S["mall_ready"], b + 1)
                act.copy(mall[:, b, :], pH1[:, 0:D + F]).then_inc(S["mall_done"], 1)

            for s in range(G + 3):
                if s < G:
                    a_hT(s)
                if 0 <= s - 1 < G:
                    a_exp(s - 1)
                if 0 <= s - 2 < G:
                    a_ft(s - 2)
                if s == GB + 3:
                    a_kv(0)
            a_kv(1)

            def a_qT(g):
                act.wait_ge(S["tq"], g + 1)
                if g >= 2:
                    act.wait_ge(S["m1_ready"], g - 1)
                act.copy(qT[:, g % 2, :], pF[:, :]).then_inc(S["qT_done"], 1)

            def a_relu(g):
                act.wait_ge(S["m1_ready"], g + 1)
                if g >= 2:
                    act.wait_ge(S["y2_ready"], g - 1)
                act.activation(hid[:, g % 2, 0, :], pH0[:, :], ACT.Relu).then_inc(S["relu0"], 1)

            def a_square(g, k, ready, done):
                act.wait_ge(S[ready], g + 1)
                if g >= 2:
                    act.wait_ge(S["yr_done"], g - 1)
                for t in range(GT):
                    last = act.activation(sqj[:, g % 2, k * GT + t, :], pQ[k][:, t * D:(t + 1) * D], ACT.Square,
                                          accum_out=ssq[:, g % 2, k * GT + t:k * GT + t + 1])
                last.then_inc(S[done], 1)

            def a_h2(g):
                b = g // GB
                act.wait_ge(S["tx3"], g + 1)
                if g >= 2:
                    act.wait_ge(S["lg_ready"], g - 1)
                act.activation(h2T[:, g % 2, :], pT[:, :], ACT.Identity, bias=colm[:, 2, b:b + 1],
                               scale=colm[:, 3, b:b + 1]).then_inc(S["h2_done"], 1)

            for s in range(G + 7):
                if 0 <= s - 6 < G:
                    a_h2(s - 6)
                if 0 <= s - 1 < G:
                    a_qT(s - 1)
                if 0 <= s - 2 < G:
                    a_square(s - 2, 0, "y1_ready", "sq1")
                    a_relu(s - 2)
                if 0 <= s - 3 < G:
                    a_square(s - 3, 1, "y2_ready", "sq2")
            act.wait_ge(S["lmax"], 1)
            act.activation(pe_[:, :, :, :].rearrange("p b e t -> p (b e t)"), m1[:, :, :, :].rearrange("p b e t -> p (b e t)"),
                           ACT.Exp).then_inc(S["exp2"], 1)
            for n in range(2 * ROUNDS):
                act.wait_ge(S["ncur_ready"], n + 1)
                keys = khi if n < ROUNDS else klo
                for j in range(DV, NC):
                    last = act.activation(junk[:, j, :], keys[:, :], ACT.Sign, bias=ncur[:, j - DV:j - DV + 1],
                                          accum_out=cnt[:, j:j + 1])
                last.then_inc(S["acounts"], 1)

            def a_xt(j, k):
                act.wait_ge(S["xt_ready"], j + 1)
                act.copy(xt[:, k % 2, :], (pT, pF)[k % 2][:, 0:P]).then_inc(S["xt_done"], 1)

            def a_w(j, k):
                e = act.value_load(eid[0:1, j], min_val=0, max_val=E - 1)
                act.copy(wcur[:, k:k + 1, 0:F], ew[:, bass.ds(e, 1), 0:F]).then_inc(S["w_done"], 1)

            def a_gelu(j, k):
                act.wait_ge(S["up_ready"], j + 1)
                act.activation(eh[:, k % 2, :], pH[k % 2][:, 0:F], ACT.Gelu).then_inc(S["eh_done"], 1)

            act.wait_ge(S["slots_done"], 1)
            act.wait_ge(S["ld_moe"], 48)
            a_w(slice(0, 1), 0)
            a_xt(0, 0)
            a_w(slice(1, 2), 1)
            with act.Fori(0, NL, R) as i:
                for k in range(R):
                    a_gelu(i + k, k)
                    a_xt(i + (k + 1), k + 1)
                    a_w(bass.ds(i + (k + 2), 1), (k + 2) % RW)
            for j in range(NL, NJ):
                a_gelu(j, j)
                if j + 1 < NJ:
                    a_xt(j + 1, j + 1)
                if j + 2 < NJ:
                    a_w(slice(j + 2, j + 3), (j + 2) % RW)

        @block.tensor
        def _(te):
            te.wait_ge(S["consts"], 1)
            te.wait_ge(S["silu_done"], 1)
            te.wait_ge(S["ld_mod"], 32)
            for n, j in enumerate((0, 1, 3, 4)):
                mm = te.matmul(pG[:, 2 * n:2 * n + 2], wmod_sb[:, j * D:(j + 1) * D], siluT[:, :], start=True, stop=True)
            mm.then_inc(S["mod_cols"], 1)
            te.wait_ge(S["silu_done"], 2)

            def p_tx(g):
                te.wait_ge(S["xn1"], g + 1)
                if g >= 1:
                    te.wait_ge(S["hT_done"], g)
                for t in range(GT):
                    mm = te.transpose(pT[:, t * P:(t + 1) * P], xn[:, g, t, :], ident[:, :])
                mm.then_inc(S["tx"], 1)

            def p_q(g):
                te.wait_ge(S["hT_done"], g + 1)
                if g >= 2:
                    te.wait_ge(S["feat_done"], g - 1)
                te.matmul(pQ[g % 2][:, :], wq[:, :], hT[:, g % 2, :], start=True, stop=True).then_inc(S["q_ready"], 1)

            def p_tf(g):
                te.wait_ge(S["feat_done"], g + 1)
                if g >= 1:
                    te.wait_ge(S["ft_done"], g)
                for t in range(GT):
                    mm = te.transpose(pF[:, t * P:(t + 1) * P], featT[:, (g * GT + t) * P:(g * GT + t + 1) * P], ident[:, :])
                mm.then_inc(S["tf"], 1)

            def p_gt(g):
                b = g // GB
                te.wait_ge(S["ft_done"], g + 1)
                for t in range(GT):
                    mm = te.matmul(pGL[b][:, 0:P], xn[:, g, t, :], feat[:, g * GT + t, :],
                                   start=(g % GB == 0 and t == 0), stop=(g % GB == GB - 1 and t == GT - 1))
                mm.then_inc(S["gt_done"], 1)

            def p_kv(b):
                te.wait_ge(S["gts_done"], b + 1)
                te.wait_ge(S["ks_done"], b + 1)
                te.wait_ge(S["rows_read"], 1)
                te.matmul(pH0[:, 0:P], wqm[:, b, :], gts[:, b, :], start=True, stop=False)
                te.matmul(pH0[:, 0:P], qbias[:, b, :], kdiag[:, b, :], start=False, stop=True).then_inc(S["kv_ready"], 1)
                te.wait_ge(S["kvt_done"], b + 1)
                if b:
                    te.wait_ge(S["mall_done"], b)
                te.matmul(pH1[:, 0:D + F], kvt[:, b, :], wmx[:, :], start=True, stop=True).then_inc(S["mall_ready"], 1)

            for s in range(G + 3):
                if s < G:
                    p_tx(s)
                if s == 0:
                    for b in range(B):
                        te.matmul(pH[b][:, 0:512], siluB[:, b, :], wmod_sb[:, 0:512], start=True, stop=True)
                    for b in range(B):
                        mm = te.matmul(pL[:, b * 256:(b + 1) * 256], siluB[:, b, :], wmod_sb[:, 512:768], start=True, stop=True)
                    mm.then_inc(S["mod_rows"], 1)
                    te.wait_ge(S["ld_attn"], 16 * 9)
                    te.transpose(pF[:, 0:P], wm[:, :], ident[:, :]).then_inc(S["wmT_ready"], 1)
                    te.wait_ge(S["cols_ready"], 1)
                    for b in range(B):
                        mm = te.matmul(pG[:, b * P:(b + 1) * P], saB[:, b, :], wq[:, :], start=True, stop=True)
                    mm.then_inc(S["qb_ready"], 1)
                if 0 <= s - 1 < G:
                    p_q(s - 1)
                if s == 1:
                    te.wait_ge(S["wmT_done"], 1)
                    te.matmul(pF[:, 0:F], wmT[:, :], w1[:, :], start=True, stop=True).then_inc(S["wmw1_ready"], 1)
                if s == 2:
                    te.wait_ge(S["wmx_done"], 1)
                if 0 <= s - 2 < G:
                    p_tf(s - 2)
                if s == 3:
                    te.wait_ge(S["prep_done"], 1)
                if 0 <= s - 3 < G:
                    if s - 3 == GB:
                        te.wait_ge(S["rows_read"], 1)
                    p_gt(s - 3)
                if s == GB + 3:
                    p_kv(0)
            p_kv(1)

            def p_den(g):
                b = g // GB
                if g >= 1:
                    te.wait_ge(S["z_done"], g)
                for t in range(GT):
                    mm = te.matmul(pG[:, t * H:(t + 1) * H], featT[:, (g * GT + t) * P:(g * GT + t + 1) * P],
                                   ksel[:, b, :], start=True, stop=True)
                mm.then_inc(S["den_ready"], 1)

            def p_tq(g):
                te.wait_ge(S["qp_done"], g + 1)
                if g >= 1:
                    te.wait_ge(S["qT_done"], g)
                for t in range(GT):
                    mm = te.transpose(pF[:, t * P:(t + 1) * P], qp[:, g % 2, t * P:(t + 1) * P], ident[:, :])
                mm.then_inc(S["tq"], 1)

            def p_y1(g):
                b = g // GB
                te.wait_ge(S["qT_done"], g + 1)
                if g % GB == 0:
                    te.wait_ge(S["mall_done"], b + 1)
                if g >= 1:
                    te.wait_ge(S["u1_done"], g)
                for t in range(GT):
                    mm = te.matmul(pQ0[:, t * D:(t + 1) * D], qT[:, g % 2, t * P:(t + 1) * P], mall[:, b, 0:D],
                                   start=True, stop=True)
                mm.then_inc(S["y1_ready"], 1)
                if g >= 1:
                    te.wait_ge(S["relu0"], g)
                    te.wait_ge(S["relu1"], g)
                for f in range(2):
                    mm = te.matmul(pH[f][:, :], mall[:, b, D + f * P:D + (f + 1) * P], qT[:, g % 2, :], start=True, stop=True)
                mm.then_inc(S["m1_ready"], 1)

            def p_y2(g):
                te.wait_ge(S["relu0"], g + 1)
                te.wait_ge(S["relu1"], g + 1)
                if g >= 1:
                    te.wait_ge(S["u2_done"], g)
                for t in range(GT):
                    for f in range(2):
                        mm = te.matmul(pQ1[:, t * D:(t + 1) * D], hid[:, g % 2, f, t * P:(t + 1) * P], w2[:, f, :],
                                       start=(f == 0), stop=(f == 1))
                mm.then_inc(S["y2_ready"], 1)

            def p_tx3(g):
                te.wait_ge(S["xn3"], g + 1)
                if g >= 1:
                    te.wait_ge(S["h2_done"], g)
                for t in range(GT):
                    mm = te.transpose(pT[:, t * P:(t + 1) * P], xn[:, g, t, :], ident[:, :])
                mm.then_inc(S["tx3"], 1)

            def p_lg(g):
                te.wait_ge(S["h2_done"], g + 1)
                for t in range(GT):
                    k = g * GT + t
                    mm = te.matmul(pL[:, k * E:(k + 1) * E], h2T[:, g % 2, t * P:(t + 1) * P], wg[:, :], start=True, stop=True)
                mm.then_inc(S["lg_ready"], 1)

            for s in range(G + 8):
                if s < G:
                    p_den(s)
                if 0 <= s - 1 < G:
                    p_tq(s - 1)
                if 0 <= s - 6 < G:
                    p_tx3(s - 6)
                if 0 <= s - 2 < G:
                    p_y1(s - 2)
                if 0 <= s - 3 < G:
                    p_y2(s - 3)
                if 0 <= s - 7 < G:
                    p_lg(s - 7)

            te.wait_ge(S["probs"], 1)
            for b in range(B):
                mm = te.transpose(pT[:, b * P:(b + 1) * P], pr[:, b, :, :].rearrange("p e t -> p (e t)"), ident[:, :])
            mm.then_inc(S["prt_ready"], 1)
            for n in range(2 * ROUNDS):
                if n:
                    te.wait_ge(S["digits"], 2 * n)
                te.matmul(pG[:, DV - 1:NC - 1], ones[:, :], c16[:, :], start=True, stop=False, skip_group_check=True)
                te.wait_ge(S["acounts"], n + 1)
                te.matmul(pG[:, DV - 1:NC - 1], half16[:, :], cnt[:, DV:NC], start=False, stop=True, skip_group_check=True)
                te.wait_ge(S["counts"], n + 1)
                te.matmul(pG[:, 0:DV - 1], same16[:, :], cnt[:, 1:DV], start=True, stop=True,
                          skip_group_check=True).then_inc(S["totals"], 1)
            te.wait_ge(S["diagT"], 1)
            te.matmul(pG[:, 0:P], ones[:, :], thd[:, :], start=True, stop=True).then_inc(S["thr_ready"], 1)
            te.wait_ge(S["gt_ready"], 1)
            te.matmul(pF[:, 0:B * P], onesb[:, :], gt_b[:, :, :, :].rearrange("p b e t -> p (b e t)"),
                      start=True, stop=True).then_inc(S["cgt_ready"], 1)
            te.wait_ge(S["rsum_ready"], 1)
            te.matmul(pL[:, 0:B * E], before[:, :], rsum[:, :, :].rearrange("p b e -> p (b e)"), start=True, stop=False,
                      skip_group_check=True)
            te.matmul(pL[:, E:2 * E], onesb[:, :], rsum[:, 0, :], start=False, stop=True,
                      skip_group_check=True).then_inc(S["base_ready"], 1)

            te.wait_ge(S["rank_ready"], 1)
            te.matmul(pL[:, 0:B * E], before[:, :], rsum[:, :, :].rearrange("p b e -> p (b e)"), start=True, stop=False,
                      skip_group_check=True)
            te.matmul(pL[:, E:2 * E], onesb[:, :], rsum[:, 0, :], start=False, stop=True, skip_group_check=True)
            for b in range(B):
                mm = te.matmul(pL[:, 2 * E:3 * E], onesb[:, :], rsum[:, b, :], start=(b == 0), stop=(b == B - 1),
                               skip_group_check=True)
            mm.then_inc(S["rbase_ready"], 1)
            for t in range(NT):
                q = t // (NT // 4)
                te.wait_ge(S["hi_ready"], q + 1)
                if q >= POOLQ:
                    te.wait_ge(S["lo_ready"], q - POOLQ + 1)
                mm = te.matmul(pG[:, 0:2 * NJ], ohlo[:, t, :], ohi[:, t, :, :].rearrange("p v j -> p (v j)"),
                               start=(t == 0), stop=(t == NT - 1))
            mm.then_inc(S["inv_ready"], 1)
            te.wait_ge(S["ohw_ready"], 1)
            for t in range(NT):
                mm = te.matmul(pL[:, 0:3 * NJ], ohlo[:, t, :], ohw[:, t, :, :].rearrange("p v j -> p (v j)"),
                               start=(t == 0), stop=(t == NT - 1))
            mm.then_inc(S["inv_ready"], 1)

            def p_xt(j, n, k):
                te.wait_ge(gathered[k % R], n)
                te.transpose((pT, pF)[k % 2][:, 0:P], row[:, k % R, 0:D], ident[:, :]).then_inc(S["xt_ready"], 1)

            def p_up(j, k):
                te.wait_ge(S["w_done"], j + 1)
                te.wait_ge(S["xt_done"], j + 1)
                for f in range(2):
                    mm = te.matmul(pH[k % 2][:, f * P:(f + 1) * P], wcur[:, k % RW, f * P:(f + 1) * P], xt[:, k % 2, :],
                                   start=True, stop=True)
                mm.then_inc(S["up_ready"], 1)

            def p_down(j, js, k):
                e = te.value_load(eid[0:1, js], min_val=0, max_val=E - 1)
                te.wait_ge(S["eh_done"], j + 1)
                te.wait_ge(S["y_free"], j + 1)
                for f in range(2):
                    mm = te.matmul(pQ[k % 2][:, 0:D], eh[:, k % 2, f * P:(f + 1) * P], ew[:, bass.ds(e, 1), F + f * D:F + (f + 1) * D],
                                   start=(f == 0), stop=(f == 1))
                mm.then_inc(S["y_ready"], 1)

            te.wait_ge(S["ld_moe"], 48)
            p_xt(0, 16, 0)
            with te.Fori(0, NL // R) as i:
                for k in range(R):
                    p_up(i * R + k, k)
                    p_xt(i * R + (k + 1), i * 16 + (16 if k < R - 1 else 32), k + 1)
                    p_down(i * R + k, bass.ds(i * R + k, 1), k)
            for j in range(NL, NJ):
                p_up(j, j)
                if j + 1 < NJ:
                    p_xt(j + 1, 16 * ((j + 1) // R + 1), j + 1)
                p_down(j, slice(j, j + 1), j)

        @block.vector
        def _(ve_):
            dve = ve_
            n = 0

            def link(ins):
                nonlocal n
                n += 1
                ins.then_inc(S["dve"], 1)
                dve.wait_ge(S["dve"], n)

            def stats(g, ready):
                for t in range(GT):
                    last = dve.bn_stats(bn[:, g, t, :], x_sb[:, g * GT + t, :])
                link(last)
                for t in range(GT):
                    last = dve.bn_aggr(mv[:, g, t, :], bn[:, g, t, :])
                return last.then_inc(S[ready], 1)

            def normalise(g):
                for t in range(GT):
                    last = dve.tensor_scalar(xn[:, g, t, :], x_sb[:, g * GT + t, :], mv[:, g, t, 0:1],
                                             rs[:, g, t:t + 1], ALU.subtract, ALU.mult)
                return last

            def v_stats1(g):
                dve.wait_ge(ld_x[g], 16)
                stats(g, "stats1")

            def v_xn1(g):
                dve.wait_ge(S["rs1"], g + 1)
                normalise(g).then_inc(S["xn1"], 1)

            def v_feat(g):
                dve.wait_ge(S["exp_done"], g + 1)
                link(dve.tensor_scalar(ex[:, g % 2, :], ex[:, g % 2, :], 1.0, None, ALU.min))
                dve.scalar_tensor_tensor(featT[:, g * W:(g + 1) * W], pQ[g % 2][:, :], 0.0, ex[:, g % 2, :], ALU.max, ALU.add,
                                         accum_out=ksp[:, g:g + 1]).then_inc(S["feat_done"], 1)

            v_stats1(0)
            dve.wait_ge(S["consts"], 1)
            dve.wait_ge(S["silu_exp"], 1)
            link(dve.tensor_scalar(ec[:, :], ec[:, :], 1.0, None, ALU.add))
            link(dve.reciprocal(ec[:, :], ec[:, :]))
            dve.wait_ge(S["ld_mod"], 32)
            dve.tensor_tensor(siluT[:, :], cT[:, :], ec[:, :], ALU.mult).then_inc(S["silu_done"], 1)
            dve.wait_ge(S["silu_done"], 1)
            v_xn1(0)
            for b in range(B):
                last = dve.tensor_scalar(siluB[:, b, :], ones[:, :], siluT[:, b:b + 1], None, ALU.mult)
            last.then_inc(S["silu_done"], 1)
            dve.wait_ge(S["mod_cols"], 1)
            link(dve.tensor_copy(colm[:, :, :].rearrange("p j b -> p (j b)"), pG[:, 0:8]))
            dve.tensor_scalar(colm[:, 1, :], colm[:, 1, :], 1.0, None, ALU.add)
            link(dve.tensor_scalar(colm[:, 3, :], colm[:, 3, :], 1.0, None, ALU.add))
            dve.tensor_scalar(saB[:, 0, :], ones[:, :], colm[:, 0, 0:1], None, ALU.mult)
            dve.tensor_scalar(saB[:, 1, :], ones[:, :], colm[:, 0, 1:2], None, ALU.mult).then_inc(S["cols_ready"], 1)
            dve.wait_ge(S["cols_ready"], 1)
            v_stats1(1)
            v_stats1(2)
            v_xn1(1)

            def prep_weights():
                dve.wait_ge(S["ld_attn"], 16 * 9)
                dve.wait_ge(S["wmT_ready"], 1)
                dve.tensor_copy(wmT[:, :], pF[:, 0:P]).then_inc(S["wmT_done"], 1)
                dve.reduce_sum(rowm[:, 0:1], wm[:, :], AX.X)
                link(dve.reduce_sum(rowm[:, 1:3], w2[:, :, :], AX.X))
                link(dve.tensor_scalar(rowm[:, 0:3], rowm[:, 0:3], -1.0 / D, None, ALU.mult))
                dve.tensor_scalar(wmx[:, 0:D], wm[:, :], rowm[:, 0:1], None, ALU.add)
                for k in range(2):
                    dve.tensor_scalar(w2[:, k, :], w2[:, k, :], rowm[:, 1 + k:2 + k], None, ALU.add)
                for b in range(B):
                    dve.tensor_scalar(wqm[:, b, :], wq[:, :], colm[:, 1, b:b + 1], None, ALU.mult)
                dve.wait_ge(S["qb_ready"], 1)
                dve.tensor_copy(qbias[:, :, :].rearrange("p b d -> p (b d)"), pG[:, 0:2 * P]).then_inc(S["prep_done"], 1)

            def prep_wmw1():
                dve.wait_ge(S["wmw1_ready"], 1)
                dve.tensor_copy(wmx[:, D:D + F], pF[:, 0:F]).then_inc(S["wmx_done"], 1)

            def prep_rows():
                dve.wait_ge(S["mod_rows"], 1)
                link(dve.tensor_tensor(bsum[:, :], rows[:, 1, :], rows[:, 3, :], ALU.add))

                def clamp(dst, v):
                    link(dve.tensor_scalar(sgn[:, :, :], v, 0.0, 2.0, ALU.is_ge, ALU.mult))
                    link(dve.scalar_tensor_tensor(dst, sgn[:, :, :], 1.0, v, ALU.subtract, ALU.mult))
                    link(dve.tensor_scalar(dst, dst, 0.25, None, ALU.max))
                    link(dve.scalar_tensor_tensor(dst, sgn[:, :, :], 1.0, dst, ALU.subtract, ALU.mult))

                lv = pL[:, :].rearrange("p (b n) -> p b n", b=B)
                for b in range(B):
                    dve.tensor_copy(modr[:, b, 0:4 * D], pH[b][:, :])
                dve.tensor_scalar(cbR[:, :, :], lv[:, :, 0:D], 1.0, None, ALU.add)
                dve.tensor_copy(modr[:, :, 4 * D:5 * D], lv[:, :, D:2 * D]).then_inc(S["rows_read"], 1)
                dve.wait_ge(S["rows_read"], 1)
                clamp(gaR[:, :, :], modr[:, :, 2 * D:3 * D])
                clamp(gbR[:, :, :], modr[:, :, 4 * D:5 * D])
                dve.tensor_copy(sbR[:, :, :], modr[:, :, 3 * D:4 * D])
                dve.tensor_tensor(dgb[:, :], gbR[:, 1, :], gbR[:, 0, :], ALU.subtract)
                link(dve.tensor_tensor(rD[:, :, :], modr[:, :, 0:D], bsum[:, :].unsqueeze(1).to_broadcast([P, B, D]), ALU.add))
                link(dve.tensor_tensor(rD[:, :, :], rD[:, :, :], gaR[:, :, :], ALU.mult))
                dve.scalar_tensor_tensor(rA[:, :, :], modr[:, :, D:2 * D], 1.0, gaR[:, :, :], ALU.add, ALU.mult)
                for dst, n in ((rB, 0), (rC, 2)):
                    last = dve.tensor_tensor(dst[:, :, :], rows[:, n, :].unsqueeze(1).to_broadcast([P, B, D]), gaR[:, :, :],
                                             ALU.mult)
                last.then_inc(S["rows_done"], 1)

            def v_ksum(b):
                dve.wait_ge(S["feat_done"], GB * (b + 1))
                link(dve.reduce_sum(ksum[:, b:b + 1], ksp[:, b * GB:(b + 1) * GB], AX.X))
                dve.tensor_scalar(ksel[:, b, :], same16[:, 0:P:HD], ksum[:, b:b + 1], None, ALU.mult)
                dve.tensor_scalar(kdiag[:, b, :], ident[:, :], ksum[:, b:b + 1], None, ALU.mult).then_inc(S["ks_done"], 1)

            def v_kvt(b):
                dve.wait_ge(S["kv_ready"], b + 1)
                dve.tensor_tensor(kvt[:, b, :], pH0[:, 0:P], same16[:, :], ALU.mult).then_inc(S["kvt_done"], 1)

            for s in range(G + 1):
                if 0 <= s - 1 < G:
                    v_feat(s - 1)
                if s + 3 < G:
                    v_stats1(s + 3)
                if s + 2 < G:
                    v_xn1(s + 2)
                if s == 0:
                    prep_weights()
                if s == 1:
                    prep_wmw1()
                    prep_rows()
                if s == GB + 1:
                    v_ksum(0)
                if s == GB + 3:
                    v_kvt(0)
            v_ksum(1)
            v_kvt(1)

            def v_z(g):
                dve.wait_ge(S["den_ready"], g + 1)
                if g >= 2:
                    dve.wait_ge(S["qp_done"], g - 1)
                link(dve.tensor_scalar(z[:, g % 2, :], pG[:, 0:GT * H], ATTN_EPS, None, ALU.add))
                dve.reciprocal(z[:, g % 2, :], z[:, g % 2, :]).then_inc(S["z_done"], 1)

            def v_relu(g):
                dve.wait_ge(S["m1_ready"], g + 1)
                if g >= 2:
                    dve.wait_ge(S["y2_ready"], g - 1)
                dve.tensor_scalar(hid[:, g % 2, 1, :], pH1[:, :], 0.0, None, ALU.max).then_inc(S["relu1"], 1)

            def v_u1(g):
                dve.wait_ge(S["sq1"], g + 1)
                dve.tensor_tensor(u1[:, g % 3], pQ0[:, :].rearrange("p (t d) -> p t d", d=D), row4(rB[:, g // GB, :]),
                                  ALU.mult).then_inc(S["u1_done"], 1)

            def v_u2(g):
                dve.wait_ge(S["sq2"], g + 1)
                dve.tensor_tensor(u2[:, g % 2], pQ1[:, :].rearrange("p (t d) -> p t d", d=D), row4(rC[:, g // GB, :]),
                                  ALU.mult).then_inc(S["u2_done"], 1)

            def v_x1(g):
                dve.wait_ge(S["yr_done"], g + 1)
                dve.wait_ge(S["acc_done"], g + 1)
                for u, n in ((u1[:, g % 3], 0), (u2[:, g % 2], GT)):
                    for t in range(GT):
                        x1 = x_sb[:, g * GT + t, :]
                        last = dve.scalar_tensor_tensor(x1, u[:, t, :], yr[:, g % 2, n + t:n + t + 1], x1, ALU.mult, ALU.add)
                    if n == 0:
                        link(last)
                last.then_inc(S["x1_done"], 1)
                dve.wait_ge(S["x1_done"], g + 1)
                stats(g, "stats3")

            def v_xn3(g):
                dve.wait_ge(S["rs3"], g + 1)
                if g == 0:
                    dve.wait_ge(S["gt_done"], G)
                normalise(g).then_inc(S["xn3"], 1)

            for s in range(G + 6):
                if s < G:
                    v_z(s)
                if 0 <= s - 5 < G:
                    v_xn3(s - 5)
                if 0 <= s - 2 < G:
                    v_relu(s - 2)
                    v_u1(s - 2)
                if 0 <= s - 4 < G:
                    v_x1(s - 4)
                if 0 <= s - 3 < G:
                    v_u2(s - 3)

            def flat(t):
                return t[:, :, :, :].rearrange("p b e t -> p (b e t)")

            def over_e(t, op, src):
                return dve.tensor_reduce(t, src.rearrange("p b e t -> p b t e"), AX.X, op)

            def b_et(t):
                return t[:, :, :].unsqueeze(2).to_broadcast([P, B, E, TB])

            def be_(t):
                return t[:, :, :].unsqueeze(3).to_broadcast([P, B, E, TB])

            def mul(o, a, b):
                return dve.tensor_tensor(o, a, b, ALU.mult)

            dve.wait_ge(S["lg_ready"], G)
            lg = pL[:, 0:NT * E].rearrange("p (b t e) -> p b e t", b=B, e=E)
            link(over_e(mx[:, :, :], ALU.max, lg))
            for b in range(B):
                last = dve.tensor_tensor(m1[:, b], lg[:, b], mx[:, b, :].unsqueeze(1).to_broadcast([P, E, TB]), ALU.subtract)
            last.then_inc(S["lmax"], 1)
            dve.wait_ge(S["exp2"], 1)
            link(over_e(sm[:, :, :], ALU.add, pe_[:, :, :, :]))
            link(dve.reciprocal(sm[:, :, :], sm[:, :, :]))
            for b in range(B):
                last = dve.tensor_tensor(pr[:, b], pe_[:, b], sm[:, b, :].unsqueeze(1).to_broadcast([P, E, TB]), ALU.mult)
            last.then_inc(S["probs"], 1)
            dve.wait_ge(S["prt_ready"], 1)
            dve.wait_ge(S["h2t_done"], G)
            link(dve.tensor_copy(prT[:, :], pT[:, 0:B * P]))
            bits = prT[:, :].bitcast(I32)
            link(dve.tensor_scalar(ki[:, :], bits, HALF, None, ALU.logical_shift_right))
            link(dve.tensor_copy(khi[:, :], ki[:, :]))
            link(dve.tensor_scalar(ki[:, :], bits, (1 << HALF) - 1, None, ALU.bitwise_and))
            link(dve.tensor_copy(klo[:, :], ki[:, :]))

            def search(keys, k):
                link(dve.tensor_scalar(cur[:, k, :], jc[:, :], steps[:, 0:1], None, ALU.mult))
                for r in range(ROUNDS):
                    n = k * ROUNDS + r
                    if n:
                        dve.wait_ge(S["totals"], n)
                    dve.tensor_scalar(ncur[:, :], cur[:, k, DV:NC], -1.0, 0.5, ALU.mult, ALU.add).then_inc(S["ncur_ready"], 1)
                    for j in range(1, DV):
                        last = dve.tensor_scalar(junk[:, j, :], keys, cur[:, k, j:j + 1], None, ALU.is_ge, ALU.add,
                                                 accum_out=cnt[:, j:j + 1])
                    last.then_inc(S["counts"], 1)
                    dve.scalar_tensor_tensor(pre[:, :], jc[:, :], steps[:, r + 1:r + 2],
                                             cur[:, k, 0:1].to_broadcast([P, NC]), ALU.mult, ALU.add)
                    dve.wait_ge(S["totals"], n + 1)
                    dve.tensor_scalar(dig[:, :], pG[:, 0:NC - 1], CAP - 0.5, None, ALU.is_ge, ALU.add,
                                      accum_out=digit[:, :]).then_inc(S["digits"], 1)
                    dve.wait_ge(S["digits"], 2 * n + 1)
                    dve.scalar_tensor_tensor(cur[:, k, :], digit[:, 0:1].to_broadcast([P, NC]),
                                             steps[:, r:r + 1], pre[:, :], ALU.mult, ALU.add).then_inc(S["digits"], 1)
                    dve.wait_ge(S["digits"], 2 * n + 2)

            search(khi[:, :], 0)
            link(dve.tensor_scalar(khi[:, :], khi[:, :], cur[:, 0, 0:1], 65536.0, ALU.subtract, ALU.mult))
            link(dve.tensor_tensor(klo[:, :], khi[:, :], klo[:, :], ALU.add))
            search(klo[:, :], 1)
            link(dve.tensor_copy(thi[:, :], cur[:, :, 0]))
            link(dve.tensor_scalar(thi[:, 0:1], thi[:, 0:1], HALF, None, ALU.logical_shift_left))
            link(dve.tensor_tensor(thi[:, 0:1], thi[:, 0:1], thi[:, 1:2], ALU.bitwise_or))
            dve.tensor_scalar(thd[:, :], ident[:, :], thi[:, 0:1].bitcast(F32), None, ALU.mult).then_inc(S["diagT"], 1)
            dve.wait_ge(S["thr_ready"], 1)
            link(dve.tensor_copy(thr[:, :], pG[:, 0:P]))
            tb = thr[:, :].unsqueeze(1).to_broadcast([P, B, P])
            pf = pr[:, :, :, :].rearrange("p b e t -> p b (e t)")
            dve.tensor_tensor(gt_b[:, :, :, :].rearrange("p b e t -> p b (e t)"), pf, tb, ALU.is_gt).then_inc(S["gt_ready"], 1)
            link(dve.tensor_tensor(eq[:, :, :, :].rearrange("p b e t -> p b (e t)"), pf, tb, ALU.is_equal))
            link(dve.tensor_tensor_scan(flat(scan), segmask[:, :], flat(eq), 0.0, ALU.mult, ALU.add))
            dve.tensor_copy(rsum[:, :, :], scan[:, :, :, TB - 1]).then_inc(S["rsum_ready"], 1)
            dve.wait_ge(S["rsum_ready"], 1)
            link(dve.tensor_tensor(flat(scan), flat(scan), flat(eq), ALU.subtract))
            dve.wait_ge(S["cgt_ready"], 1)
            link(dve.tensor_reduce(base[:, :, :], pF[:, 0:B * P].rearrange("p (b e t) -> p b e t", b=B, e=E), AX.X, ALU.add))
            link(dve.tensor_tensor(cgt[:, :], base[:, 0, :], base[:, 1, :], ALU.add))
            dve.wait_ge(S["base_ready"], 1)
            link(dve.tensor_tensor(base[:, :, :], pL[:, 0:B * E].rearrange("p (b e) -> p b e", b=B),
                                   cgt[:, :].unsqueeze(1).to_broadcast([P, B, E]), ALU.add))
            for b in range(B):
                last = dve.tensor_tensor(m1[:, b], scan[:, b], base[:, b, :].unsqueeze(2).to_broadcast([P, E, TB]), ALU.add)
            link(last)
            link(dve.scalar_tensor_tensor(flat(m2), flat(m1), CAP - 0.5, flat(eq), ALU.is_lt, ALU.mult))
            link(dve.tensor_tensor(flat(sel), flat(m2), flat(gt_b), ALU.add))
            link(over_e(anys[:, :, :], ALU.max, sel[:, :, :, :]))
            for b in range(B):
                last = dve.scalar_tensor_tensor(m1[:, b], sel[:, b], 1.0, anys[:, b, :].unsqueeze(1).to_broadcast([P, E, TB]),
                                                ALU.subtract, ALU.mult)
            link(last)
            link(dve.scalar_tensor_tensor(flat(m1), flat(m1), 2.0, flat(pr), ALU.mult, ALU.add))
            link(over_e(mx[:, :, :], ALU.max, m1[:, :, :, :]))
            for b in range(B):
                last = dve.tensor_tensor(m2[:, b], m1[:, b], mx[:, b, :].unsqueeze(1).to_broadcast([P, E, TB]), ALU.is_lt)
            link(last)
            for b in range(B):
                last = dve.scalar_tensor_tensor(m2[:, b], m2[:, b], float(E), eidx[:, :].unsqueeze(2).to_broadcast([P, E, TB]),
                                                ALU.mult, ALU.add)
            link(last)
            link(over_e(sm[:, :, :], ALU.min, m2[:, :, :, :]))
            for b in range(B):
                last = dve.tensor_tensor(m1[:, b], m2[:, b], sm[:, b, :].unsqueeze(1).to_broadcast([P, E, TB]), ALU.is_equal)
            link(last)
            oh = m1
            link(dve.tensor_tensor_scan(flat(scan), segmask[:, :], flat(oh), 0.0, ALU.mult, ALU.add))
            dve.tensor_copy(rsum[:, :, :], scan[:, :, :, TB - 1]).then_inc(S["rank_ready"], 1)
            wt = mx[:, :, :].rearrange("p b t -> p (b t)")
            dve.wait_ge(S["rbase_ready"], 1)
            link(dve.tensor_copy(tot[:, :], pL[:, 2 * E:3 * E]))
            link(dve.tensor_scalar(toti[:, :], tot[:, :], float(P - 1), None, ALU.add))
            link(dve.tensor_scalar(toti[:, :], toti[:, :], 7, None, ALU.logical_shift_right))
            link(dve.tensor_copy(ntile[:, :], toti[:, :]))
            link(dve.tensor_tensor_scan(tend[:, :], ones[:, 0:E], ntile[:, :], 0.0, ALU.mult, ALU.add))
            link(dve.tensor_tensor(tot[:, :], tend[:, :], ntile[:, :], ALU.subtract))
            for b in range(B):
                last = dve.scalar_tensor_tensor(base[:, b, :], tot[:, :], float(P), pL[:, b * E:(b + 1) * E], ALU.mult, ALU.add)
            link(last)
            for b in range(B):
                last = dve.tensor_tensor(m2[:, b], scan[:, b], base[:, b, :].unsqueeze(2).to_broadcast([P, E, TB]), ALU.add)
            link(last)
            link(dve.tensor_tensor(flat(m2), flat(m2), flat(oh), ALU.mult))
            link(over_e(sm[:, :, :], ALU.add, m2[:, :, :, :]))
            link(dve.tensor_scalar(posi[:, :], sm[:, :, :].rearrange("p b t -> p (b t)"), -1.0, None, ALU.add))
            dve.tensor_scalar(loi[:, :], posi[:, :], P - 1, None, ALU.bitwise_and)
            link(dve.tensor_scalar(hii[:, :], posi[:, :], 7, None, ALU.logical_shift_right))
            dve.tensor_copy(lo[:, :], loi[:, :])
            dve.tensor_copy(hi[:, :], hii[:, :]).then_inc(S["slot_ready"], 1)
            dve.wait_ge(S["slot_ready"], 1)
            nq = NT // 4
            for q in range(4):
                ts = slice(q * nq, (q + 1) * nq)
                if q < POOLQ:
                    dve.tensor_tensor(ohlo[:, ts, :], iota[:, :].unsqueeze(1).to_broadcast([P, nq, P]),
                                      lo[:, ts].unsqueeze(2).to_broadcast([P, nq, P]), ALU.is_equal)
                link(dve.tensor_tensor(ohhi[:, ts, :], iotaj[:, 0:NJ].unsqueeze(1).to_broadcast([P, nq, NJ]),
                                       hi[:, ts].unsqueeze(2).to_broadcast([P, nq, NJ]), ALU.is_equal))
                for v in range(2):
                    last = dve.tensor_tensor(ohi[:, ts, v, :], ohhi[:, ts, :],
                                             val[:, v, ts].unsqueeze(2).to_broadcast([P, nq, NJ]), ALU.mult)
                last.then_inc(S["hi_ready"], 1)
            link(dve.tensor_tensor(ecmp[:, :, :], iotaj[:, :].unsqueeze(2).to_broadcast([P, NJ + 2, E]),
                                   tend[:, :].unsqueeze(1).to_broadcast([P, NJ + 2, E]), ALU.is_ge))
            link(dve.tensor_reduce(eidf[:, :], ecmp[:, :, :], AX.X, ALU.add))
            link(dve.tensor_scalar(eid[:, :], eidf[:, :], float(E - 1), None, ALU.min))
            dve.wait_ge(S["inv_ready"], 1)
            link(dve.tensor_copy(inv[:, 0:2, :].rearrange("p v j -> p (v j)"), pG[:, 0:2 * NJ]))
            link(dve.scalar_tensor_tensor(idf[:, :], inv[:, 0, :], -1.0, inv[:, 1, :], ALU.add, ALU.add))
            dve.tensor_scalar(gidx[:, :], idf[:, :], 0.0, None, ALU.max)
            link(dve.tensor_scalar(oob[:, :], idf[:, :], 0.0, float(2 * B * L), ALU.is_lt, ALU.mult))
            dve.tensor_tensor(sidx[:, :], idf[:, :], oob[:, :], ALU.add).then_inc(S["slots_done"], 1)
            dve.tensor_scalar(flag[:, :], idf[:, :], float(L), None, ALU.is_ge)
            link(dve.tensor_copy(val[:, 2, :], wt))
            link(dve.tensor_tensor(lo[:, :], wt, val[:, 2, :], ALU.subtract))
            link(dve.tensor_copy(val[:, 3, :], lo[:, :]))
            link(dve.tensor_tensor(hi[:, :], lo[:, :], val[:, 3, :], ALU.subtract))
            link(dve.tensor_copy(val[:, 4, :], hi[:, :]))
            for v in range(3):
                last = dve.tensor_tensor(ohw[:, :, v, :], ohhi[:, :, :], val[:, 2 + v, :].unsqueeze(2).to_broadcast([P, NT, NJ]),
                                         ALU.mult)
            last.then_inc(S["ohw_ready"], 1)
            dve.wait_ge(S["inv_ready"], 2)
            link(dve.tensor_copy(inv[:, 2:5, :].rearrange("p v j -> p (v j)"), pL[:, 0:3 * NJ]))
            link(dve.tensor_tensor(wslot[:, :], inv[:, 4, :], inv[:, 3, :], ALU.add))
            link(dve.tensor_tensor(wslot[:, :], wslot[:, :], inv[:, 2, :], ALU.add))
            dve.wait_ge(S["slots_done"], 1)

            def finish(j, n, js, k):
                dve.scalar_tensor_tensor(gsel[:, k % 4, :], dgb[:, :], flag[:, js], gbR[:, 0, :], ALU.mult, ALU.add)\
                   .then_inc(S["gsel_done"], 1)
                dve.wait_ge(S["y_ready"], j + 1)
                dve.wait_ge(S["gsel_done"], j + 1)
                dve.scalar_tensor_tensor(yw[:, k % 4, :], pQ[k % 2][:, 0:D], wslot[:, js], gsel[:, k % 4, :], ALU.mult, ALU.mult)\
                   .then_inc(S["y_free"], 1)
                dve.wait_ge(S["y_free"], j + 3)
                if n is not None:
                    dve.wait_ge(scattered[k % R], n)
                dve.tensor_tensor(o_sb[:, k % R, :], yw[:, k % 4, :], row[:, k % R, D:2 * D], ALU.add).then_inc(S["o_done"], 1)

            for k in range(2):
                dve.memset(dig[:, k:k + 1], 0.0).then_inc(S["y_free"], 1)
            for j in range(R):
                finish(j, None, slice(j, j + 1), j)
            with dve.Fori(1, NL // R) as i:
                for k in range(R):
                    finish(i * R + k, i * 16, bass.ds(i * R + k, 1), k)
            for j in range(NL, NJ):
                finish(j, 16 * (j // R), slice(j, j + 1), j)


_INS = ['L0_attn_x', 'L0_attn_Wq', 'L0_attn_Wm', 'L0_attn_W1', 'L0_attn_W2', 'L0_attn_g1', 'L0_attn_b1', 'L0_attn_g2',
        'L0_attn_b2', 'L0_ffn_Wg', 'L0_ffn_W1', 'L0_ffn_W2', 'L0_c', 'L0_wmod']


def kernel(**inputs):
    import numpy as _np
    import concourse.bacc as _bacc
    from concourse import mybir as _mybir
    from concourse.bass_utils import run_bass_kernel_spmd as _run

    nc = _bacc.Bacc("TRN2", target_bir_lowering=False, num_devices=1)
    arrays, args = {}, []
    for name in _INS:
        a = _np.ascontiguousarray(inputs[name])
        arrays[f"in_{name}_dram"] = a
        args.append(nc.dram_tensor(f"in_{name}_dram", a.shape, _mybir.dt.from_np(a.dtype), kind="ExternalInput").ap())
    table = nc.dram_tensor("table_dram", (B * L, 2 * D), F32, kind="Internal").ap()
    out = nc.dram_tensor("out_dram", (B, L, D), F32, kind="ExternalOutput").ap()
    build(nc, *args, table, out)
    r = _run(nc, [arrays], core_ids=[0])
    return r.results[0]["out_dram"]
```

```python
from contextlib import ExitStack

import concourse.bass as bass
from concourse import mybir

F32 = mybir.dt.float32
BF16 = mybir.dt.bfloat16
I32 = mybir.dt.int32
ALU = mybir.AluOpType
ACT = mybir.ActivationFunctionType
AX = mybir.AxisListType

P = 128
B, L, D = 2, 2048, 128
H, HD = 8, 16
E, F = 8, 256
CAP = B * L // E
TB = L // P
NT = B * TB
GT = 4
G = NT // GT
GB = G // B
W = GT * P
LN_EPS = 1e-5
ATTN_EPS = 1e-6
BITS = 3
HALF = 15
ROUNDS = HALF // BITS
NC = 2 ** BITS
DV = 5
EARLY = 4
NJ = NT + E - 1
R = 12
RW = 4
POOLQ = 3
NL = NJ // R * R


def build(nc, x, Wq, Wm, W1, W2, g1, b1, g2, b2, Wg, EW1, EW2, c, wmod, table, out):
    with ExitStack() as ctx:
        def sb(name, shape, dt=F32):
            return ctx.enter_context(nc.sbuf_tensor(name, shape, dt))

        def psum(name):
            return ctx.enter_context(nc.psum_tensor(name, [P, 512], F32))

        def sem(name):
            return ctx.enter_context(nc.semaphore(name))

        x_sb = sb("x_sb", [P, NT, D])
        featT = sb("featT", [P, NT * P])
        feat = sb("feat", [P, NT, D])
        h2 = sb("h2", [P, NT, D])
        ew = sb("ew", [P, E, 2 * F])

        wq = sb("wq", [P, D]); wm = sb("wm", [P, D]); w1 = sb("w1", [P, F]); w2 = sb("w2", [P, 2, D])
        wg = sb("wg", [P, E]); wmod_sb = sb("wmod_sb", [P, 6 * D]); cT = sb("cT", [P, B])
        rows = sb("rows", [P, 4, D])
        wmT = sb("wmT", [P, D])
        wmx = sb("wmx", [P, D + F])
        wqm = sb("wqm", [P, B, D])
        qbias = sb("qbias", [P, B, D])

        ident = sb("ident", [P, P]); ones = sb("ones", [P, P]); same16 = sb("same16", [P, P])
        before = sb("before", [P, P], BF16); onesb = sb("onesb", [P, P], BF16)
        neghalf = sb("neghalf", [P, 8]); steps = sb("steps", [P, ROUNDS + 1]); jc = sb("jc", [P, NC])
        half16 = sb("half16", [P, P]); c16 = sb("c16", [P, NC - DV]); iota = sb("iota", [P, P], BF16)
        iotaj = sb("iotaj", [P, NJ])
        eidx = sb("eidx", [P, E]); segmask = sb("segmask", [P, NT * E])

        ec = sb("ec", [P, B]); siluT = sb("siluT", [P, B]); siluB = sb("siluB", [P, B, P])
        colm = sb("colm", [P, 4, B])
        saB = sb("saB", [P, B, P])
        gaR = sb("gaR", [P, B, D]); gbR = sb("gbR", [P, B, D]); sgn = sb("sgn", [P, B, D]); modr = sb("modr", [P, B, 5 * D])
        rA = sb("rA", [P, B, D]); rB = sb("rB", [P, B, D]); rC = sb("rC", [P, B, D]); rD = sb("rD", [P, B, D])
        cbR = sb("cbR", [P, B, D]); dgb = sb("dgb", [P, D])
        bsum = sb("bsum", [P, D]); rowm = sb("rowm", [P, 4])

        bn = sb("bn", [P, G, GT, 6]); mv = sb("mv", [P, G, GT, 2]); ve = sb("ve", [P, G, GT]); rs = sb("rs", [P, G, GT])
        xn = sb("xn", [P, G, GT, D]); h2T = sb("h2T", [P, 2, W]); hT = sb("hT", [P, 2, W]); ex = sb("ex", [P, 2, W])
        ksp = sb("ksp", [P, G]); ksum = sb("ksum", [P, B]); ksel = sb("ksel", [P, B, H]); kdiag = sb("kdiag", [P, B, P])
        gts = sb("gts", [P, B, P]); kvt = sb("kvt", [P, B, P]); mall = sb("mall", [P, B, D + F])
        z = sb("z", [P, 2, GT * H]); qp = sb("qp", [P, 2, W]); qT = sb("qT", [P, 2, W])
        hid = sb("hid", [P, 2, 2, W]); ssq = sb("ssq", [P, 2, 2 * GT]); yv = sb("yv", [P, 2, 2 * GT]); yr = sb("yr", [P, 2, 2 * GT])
        u1 = sb("u1", [P, 3, GT, D]); u2 = sb("u2", [P, 2, GT, D]); t2 = sb("t2", [P, GT, D]); t1 = sb("t1", [P, GT, D])
        sqj = sb("sqj", [P, 2, 2 * GT, D], BF16)

        mx = sb("mx", [P, B, TB]); pr = sb("pr", [P, B, E, TB]); pe_ = sb("pe_", [P, B, E, TB]); sm = sb("sm", [P, B, TB])
        prT = sb("prT", [P, B * P]); khi = sb("khi", [P, B * P]); ki = sb("ki", [P, B * P], I32); klo = sb("klo", [P, B * P])
        cur = sb("cur", [P, 2, NC]); pre = sb("pre", [P, NC]); cnt = sb("cnt", [P, NC]); dig = sb("dig", [P, NC - 1])
        thr0 = sb("thr0", [P, 1])
        digit = sb("digit", [P, 1]); thi = sb("thi", [P, 2], I32); thd = sb("thd", [P, P]); thr = sb("thr", [P, P])
        gt_b = sb("gt_b", [P, B, E, TB], BF16); eq = sb("eq", [P, B, E, TB]); scan = sb("scan", [P, B, E, TB])
        rsum = sb("rsum", [P, B, E], BF16); base = sb("base", [P, B, E]); cgt = sb("cgt", [P, E])
        sel = sb("sel", [P, B, E, TB]); m1 = sb("m1", [P, B, E, TB]); m2 = sb("m2", [P, B, E, TB]); anys = sb("anys", [P, B, TB])
        tot = sb("tot", [P, E]); toti = sb("toti", [P, E], I32); ntile = sb("ntile", [P, E]); tend = sb("tend", [P, E])
        posi = sb("posi", [P, NT], I32); loi = sb("loi", [P, NT], I32); hii = sb("hii", [P, NT], I32)
        lo = sb("lo", [P, NT]); hi = sb("hi", [P, NT])
        val = sb("val", [P, 5, NT], BF16)
        inv = sb("inv", [P, 5, NJ]); idf = sb("idf", [P, NJ]); oob = sb("oob", [P, NJ])
        gidx = sb("gidx", [P, NJ], I32)
        sidx = sb("sidx", [P, NJ], I32)
        flag = sb("flag", [P, NJ]); wslot = sb("wslot", [P, NJ])
        eidf = sb("eidf", [P, NJ]); eid = sb("eid", [P, NJ], I32)

        spaces = {"featT": featT[:, :], "feat": feat[:, :, :].rearrange("p t d -> p (t d)"),
                  "xn": xn[:, :, :, :].rearrange("p g t d -> p (g t d)")}
        used = dict.fromkeys(spaces, 0)

        def take(name, width):
            at = used[name]
            used[name] = at + width
            return spaces[name][:, at:at + width]

        def bf16(words, width, *dims):
            v = words.bitcast(BF16)
            return v.rearrange("p (t c) -> p t c", c=width) if not dims else v.rearrange("p (t v c) -> p t v c", v=dims[0], c=width)

        ohlo = bf16(take("featT", NT * P // 2), P)
        ohhi = bf16(take("feat", NT * NJ // 2), NJ)
        ohi = bf16(take("feat", NT * 2 * NJ // 2), NJ, 2)
        ohw = bf16(take("featT", NT * 3 * NJ // 2), NJ, 3)
        ecmp = take("feat", NJ * E).rearrange("p (j e) -> p j e", e=E)
        row = take("xn", R * 2 * D).rearrange("p (k c) -> p k c", c=2 * D)
        o_sb = u1[:, :, :, :].rearrange("p a t d -> p (a t) d")
        junk = hT[:, :, :].rearrange("p a c -> p (a c)").bitcast(BF16).rearrange("p (n c) -> p n c", c=B * P)
        wcur = hid[:, :, :, 0:F].rearrange("p a f c -> p (a f) c")
        eh = u2[:, 0, :, :].rearrange("p (k a) d -> p k (a d)", k=2)
        xt = u2[:, 1, 0:2, :]
        gsel, yw = (qp[:, n, :].rearrange("p (k d) -> p k d", d=D) for n in range(2))

        pT, pF, pQ0, pQ1, pH0, pH1, pG, pL = (psum(n) for n in ("pT", "pF", "pQ0", "pQ1", "pH0", "pH1", "pG", "pL"))
        pQ, pH, pGL = (pQ0, pQ1), (pH0, pH1), (pG, pL)

        names = """ld_c ld_mod ld_attn ld_moe consts
            silu_exp silu_done mod_cols cols_ready mod_rows rows_read wmT_ready wmT_done wmw1_ready wmx_done qb_ready prep_done rows_done
            stats1 rs1 xn1 tx hT_done q_ready neg_done exp_done feat_done tf ft_done gt_done acc_done
            ks_done gts_done kv_ready kvt_done mall_ready mall_done
            den_ready z_done qp_done tq qT_done y1_ready m1_ready relu0 relu1 y2_ready sq1 sq2 u1_done u2_done yr_done x1_done
            stats3 rs3 xn3 tx3 h2_done lg_ready
            lmax exp2 probs prt_ready counts totals keys diagT thr_ready gt_ready cgt_ready rsum_ready base_ready
            tab_done h2t_done acounts
            rank_ready rbase_ready slot_ready lo_ready hi_ready inv_ready ohw_ready slots_done
            w_done xt_ready xt_done up_ready eh_done y_ready y_free gsel_done o_done digits dve pool""".split()
        S = {n: sem(n) for n in names}
        ld_x = [sem(f"ld_x{g}") for g in range(G)]
        gathered = [sem(f"gathered{k}") for k in range(R)]
        scattered = [sem(f"scattered{k}") for k in range(R)]

        block = ctx.enter_context(nc.Block())

        def bgroup(t, g):
            return t[:, g * GT:(g + 1) * GT, :]

        def row4(r):
            return r.unsqueeze(1).to_broadcast([P, GT, D])

        @block.sync
        def _(sp):
            xv = x.rearrange("b (p t) d -> b p t d", p=P)
            tv = table.rearrange("(b p t) c -> b p t c", b=B, p=P)
            sp.dma_start(bgroup(x_sb, 0), xv[0, :, 0:GT, :]).then_inc(ld_x[0], 16)
            sp.dma_start(wmod_sb[:, :], wmod).then_inc(S["ld_mod"], 16)
            weights = [(wq[:, :], Wq), (wm[:, :], Wm), (w1[:, :], W1), (w2[:, :, :], W2.rearrange("(k p) d -> p k d", p=P))]
            for g in range(1, G):
                t0 = g % GB * GT
                if g > 1 and weights:
                    dst, src = weights.pop(0)
                    sp.dma_start(dst, src).then_inc(S["ld_attn"], 16)
                sp.dma_start(bgroup(x_sb, g), xv[g // GB, :, t0:t0 + GT, :]).then_inc(ld_x[g], 16)
            sp.dma_start(ew[:, :, 0:F], EW1.rearrange("e d f -> d e f")).then_inc(S["ld_moe"], 16)
            for k in range(2):
                sp.dma_start(ew[:, :, F + k * D:F + (k + 1) * D], EW2.rearrange("e (k p) d -> k p e d", p=P)[k]).then_inc(S["ld_moe"], 16)
            for g in range(G):
                t0 = g % GB * GT
                sp.wait_ge(S["x1_done"], g + 1)
                sp.dma_start(tv[g // GB, :, t0:t0 + GT, D:2 * D], bgroup(x_sb, g)).then_inc(S["tab_done"], 16)
                sp.wait_ge(S["h2t_done"], g + 1)
                sp.dma_start(tv[g // GB, :, t0:t0 + GT, 0:D], bgroup(h2, g)).then_inc(S["tab_done"], 16)
            for k in range(R):
                sp.wait_ge(scattered[k], 16 * ((NJ - 1 - k) // R + 1))

        @block.gpsimd
        def _(gp):
            n = 0

            def link(ins):
                nonlocal n
                n += 1
                ins.then_inc(S["pool"], 1)
                gp.wait_ge(S["pool"], n)

            gp.memset(ident[:, :], 0.0)
            gp.memset(ones[:, :], 1.0)
            gp.memset(onesb[:, :], 1.0)
            gp.memset(same16[:, :], 1.0)
            gp.memset(before[:, :], 1.0)
            gp.memset(neghalf[:, :], -0.5)
            gp.memset(segmask[:, :], 1.0)
            gp.memset(half16[:, :], -0.5)
            gp.memset(c16[:, :], float(NT // 2))
            for k in range(ROUNDS + 1):
                gp.memset(steps[:, k:k + 1], float(NC) ** (ROUNDS - 1 - k))
            for k in range(NC):
                gp.memset(jc[:, k:k + 1], float(k))
            link(gp.memset(rowm[:, 0:1], 0.0))
            gp.affine_select(out=ident[:, :], in_=ident[:, :], compare_op=ALU.not_equal, fill=1.0, base=0,
                             pattern=[[-1, P]], channel_multiplier=1)
            gp.affine_select(out=before[:, :], in_=before[:, :], compare_op=ALU.is_gt, fill=0.0, base=0,
                             pattern=[[1, P]], channel_multiplier=-1)
            gp.affine_select(out=segmask[:, :], in_=segmask[:, :], compare_op=ALU.not_equal, fill=0.0, base=0,
                             pattern=[[0, B * E], [1, TB]], channel_multiplier=0)
            gp.iota(eidx[:, :], pattern=[[1, E]], base=0, channel_multiplier=0, allow_small_or_imprecise_dtypes=True)
            gp.iota(iota[:, :], pattern=[[1, P]], base=0, channel_multiplier=0, allow_small_or_imprecise_dtypes=True)
            gp.iota(iotaj[:, :], pattern=[[1, NJ]], base=0, channel_multiplier=0, allow_small_or_imprecise_dtypes=True)
            for b in range(B):
                gp.iota(val[:, 0, b * TB:(b + 1) * TB], pattern=[[0, TB]], base=b * L, channel_multiplier=TB,
                        allow_small_or_imprecise_dtypes=True)
                gp.iota(val[:, 1, b * TB:(b + 1) * TB], pattern=[[1, TB]], base=1, channel_multiplier=0,
                        allow_small_or_imprecise_dtypes=True)
            for m in (half16, same16):
                blocks = m[:, :].rearrange("p (h c) -> p h c", c=HD)
                link(gp.affine_select(out=blocks, in_=blocks, compare_op=ALU.is_ge, fill=0.0, base=0,
                                      pattern=[[-HD, H], [0, HD]], channel_multiplier=1))
                last = gp.affine_select(out=blocks, in_=blocks, compare_op=ALU.is_ge, fill=0.0, base=HD - 1,
                                        pattern=[[HD, H], [0, HD]], channel_multiplier=-1)
            last.then_inc(S["consts"], 1)

            def rsqrt(dst, src, tmp, scale, eps, width):
                link(gp.tensor_scalar(tmp, src, scale, eps, ALU.mult, ALU.add))
                return gp.tensor_tensor(dst, tmp, neghalf[:, 0:width], ALU.pow)

            def rs_a(g):
                gp.wait_ge(S["stats1"], g + 1)
                rsqrt(rs[:, g, :], mv[:, g, :, 1], ve[:, g, :], 1.0, LN_EPS, GT).then_inc(S["rs1"], 1)

            def acc(g):
                b = g // GB
                gp.wait_ge(S["xn1"], g + 1)
                if g:
                    gp.wait_ge(S["acc_done"], g)
                link(gp.tensor_tensor(t1[:, :, :], xn[:, g], row4(rA[:, b, :]), ALU.mult))
                link(gp.tensor_tensor(t1[:, :, :], t1[:, :, :], row4(rD[:, b, :]), ALU.add))
                gp.tensor_tensor(bgroup(x_sb, g), bgroup(x_sb, g), t1[:, :, :], ALU.add).then_inc(S["acc_done"], 1)

            for g in range(G):
                rs_a(g)
            gp.wait_ge(S["rows_done"], 1)
            for g in range(EARLY):
                acc(g)

            def qprime(g):
                gp.wait_ge(S["z_done"], g + 1)
                if g >= 2:
                    gp.wait_ge(S["tq"], g - 1)
                gp.wait_ge(S["ft_done"], g + 1)
                gp.tensor_tensor(qp[:, g % 2, :].rearrange("p (t c) -> p t c", c=HD),
                                 bgroup(feat, g).rearrange("p t (h c) -> p (t h) c", c=HD),
                                 z[:, g % 2, :].unsqueeze(2).to_broadcast([P, GT * H, HD]), ALU.mult).then_inc(S["qp_done"], 1)

            def yrs(g):
                gp.wait_ge(S["sq1"], g + 1)
                gp.wait_ge(S["sq2"], g + 1)
                if g >= 2:
                    gp.wait_ge(S["x1_done"], g - 1)
                rsqrt(yr[:, g % 2, :], ssq[:, g % 2, :], yv[:, g % 2, :], 1.0 / D, LN_EPS, 2 * GT).then_inc(S["yr_done"], 1)

            def rs3(g):
                gp.wait_ge(S["stats3"], g + 1)
                rsqrt(rs[:, g, :], mv[:, g, :, 1], ve[:, g, :], 1.0, LN_EPS, GT).then_inc(S["rs3"], 1)

            def h2tok(g):
                gp.wait_ge(S["xn3"], g + 1)
                if g:
                    gp.wait_ge(S["h2t_done"], g)
                link(gp.tensor_tensor(t2[:, :, :], xn[:, g], row4(cbR[:, g // GB, :]), ALU.mult))
                gp.tensor_tensor(bgroup(h2, g), t2[:, :, :], row4(modr[:, g // GB, 3 * D:4 * D]), ALU.add).then_inc(S["h2t_done"], 1)

            for s in range(G + 6):
                if s < G:
                    qprime(s)
                if 0 <= s - 4 < G:
                    rs3(s - 4)
                if 0 <= s - 3 < G:
                    yrs(s - 3)
                if EARLY <= s - 2 < G:
                    acc(s - 2)
            for g in range(G):
                h2tok(g)

            gp.wait_ge(S["slot_ready"], 1)
            nq = NT // 4
            for q in range(POOLQ, 4):
                for t in range(q * nq, (q + 1) * nq):
                    last = gp.tensor_scalar(ohlo[:, t, :], iota[:, :], lo[:, t:t + 1], None, ALU.is_equal)
                last.then_inc(S["lo_ready"], 1)
            gp.wait_ge(S["slots_done"], 1)
            gp.wait_ge(S["tab_done"], 16 * 2 * G)

            def gather(j):
                gp.indirect_dma_start(row[:, j % R, :], None, table[:, :], bass.IndirectOffsetOnAxis(gidx[:, j:j + 1], 0),
                                      bounds_check=B * L - 1, oob_is_err=False).then_inc(gathered[j % R], 16)

            def scatter(j):
                gp.indirect_dma_start(out.rearrange("b l d -> (b l) d"), bass.IndirectOffsetOnAxis(sidx[:, j:j + 1], 0),
                                      o_sb[:, j % R, :], None, bounds_check=B * L - 1, oob_is_err=False).then_inc(scattered[j % R], 16)

            for k in range(R):
                gather(k)
            for j in range(NJ):
                gp.wait_ge(S["o_done"], j + 1)
                scatter(j)
                if j + R < NJ:
                    gather(j + R)

        @block.scalar
        def _(act):
            n = 0
            act.dma_start(cT[:, :], c.rearrange("b d -> d b"), allow_slow_non_contiguous=True).then_inc(S["ld_c"], 16)
            act.dma_start(wg[:, :], Wg).then_inc(S["ld_attn"], 16)
            for n, r in enumerate((g1, b1, g2, b2)):
                act.dma_start(rows[:, n, :], r.partition_broadcast(P)).then_inc(S["ld_attn"], 16)
            act.wait_ge(S["ld_c"], 16)
            act.activation(ec[:, :], cT[:, :], ACT.Exp, scale=-1.0).then_inc(S["silu_exp"], 1)
            act.wait_ge(S["cols_ready"], 1)

            def a_hT(g):
                b = g // GB
                act.wait_ge(S["tx"], g + 1)
                if g >= 2:
                    act.wait_ge(S["q_ready"], g - 1)
                act.activation(hT[:, g % 2, :], pT[:, :], ACT.Identity, bias=colm[:, 0, b:b + 1],
                               scale=colm[:, 1, b:b + 1]).then_inc(S["hT_done"], 1)

            def a_exp(g):
                act.wait_ge(S["q_ready"], g + 1)
                if g >= 2:
                    act.wait_ge(S["feat_done"], g - 1)
                act.activation(ex[:, g % 2, :], pQ[g % 2][:, :], ACT.Relu, scale=-1.0).then_inc(S["neg_done"], 1)
                act.wait_ge(S["neg_done"], g + 1)
                act.activation(ex[:, g % 2, :], ex[:, g % 2, :], ACT.Exp, scale=-1.0).then_inc(S["exp_done"], 1)

            def a_ft(g):
                act.wait_ge(S["tf"], g + 1)
                act.copy(bgroup(feat, g), pF[:, :].rearrange("p (t d) -> p t d", d=D)).then_inc(S["ft_done"], 1)

            def a_gts(b):
                act.wait_ge(S["gt_done"], GB * (b + 1))
                act.copy(gts[:, b, :], pGL[b][:, 0:P]).then_inc(S["gts_done"], 1)

            def a_mall(b):
                act.wait_ge(S["mall_ready"], b + 1)
                act.copy(mall[:, b, :], pH1[:, 0:D + F]).then_inc(S["mall_done"], 1)

            for s in range(G + 3):
                if s < G:
                    a_hT(s)
                if s == 0:
                    act.wait_ge(S["mod_rows"], 1)
                    lv = pL[:, :].rearrange("p (b n) -> p b n", b=B)
                    for b in range(B):
                        act.copy(modr[:, b, 0:4 * D], pH[b][:, :])
                    act.activation(cbR[:, :, :], lv[:, :, 0:D], ACT.Identity, bias=ones[:, 0:1])
                    act.copy(modr[:, :, 4 * D:5 * D], lv[:, :, D:2 * D]).then_inc(S["rows_read"], 1)
                if 0 <= s - 1 < G:
                    a_exp(s - 1)
                if 0 <= s - 2 < G:
                    a_ft(s - 2)
                if s == GB + 3:
                    a_gts(0)
                    a_mall(0)
            a_gts(1)

            def a_qT(g):
                act.wait_ge(S["tq"], g + 1)
                if g >= 2:
                    act.wait_ge(S["m1_ready"], g - 1)
                act.copy(qT[:, g % 2, :], pF[:, :]).then_inc(S["qT_done"], 1)

            def a_relu(g):
                act.wait_ge(S["m1_ready"], g + 1)
                if g >= 2:
                    act.wait_ge(S["y2_ready"], g - 1)
                act.activation(hid[:, g % 2, 0, :], pH0[:, :], ACT.Relu).then_inc(S["relu0"], 1)

            def a_square(g, k, ready, done):
                act.wait_ge(S[ready], g + 1)
                if g >= 2:
                    act.wait_ge(S["yr_done"], g - 1)
                for t in range(GT):
                    last = act.activation(sqj[:, g % 2, k * GT + t, :], pQ[k][:, t * D:(t + 1) * D], ACT.Square,
                                          accum_out=ssq[:, g % 2, k * GT + t:k * GT + t + 1])
                last.then_inc(S[done], 1)

            def a_h2(g):
                b = g // GB
                act.wait_ge(S["tx3"], g + 1)
                if g >= 2:
                    act.wait_ge(S["lg_ready"], g - 1)
                act.activation(h2T[:, g % 2, :], pT[:, :], ACT.Identity, bias=colm[:, 2, b:b + 1],
                               scale=colm[:, 3, b:b + 1]).then_inc(S["h2_done"], 1)

            for s in range(G + 7):
                if 0 <= s - 6 < G:
                    a_h2(s - 6)
                if 0 <= s - 1 < G:
                    a_qT(s - 1)
                if s == 1:
                    a_mall(1)
                if 0 <= s - 2 < G:
                    a_square(s - 2, 0, "y1_ready", "sq1")
                    a_relu(s - 2)
                if 0 <= s - 3 < G:
                    a_square(s - 3, 1, "y2_ready", "sq2")
            act.wait_ge(S["lmax"], 1)
            act.activation(pe_[:, :, :, :].rearrange("p b e t -> p (b e t)"), m1[:, :, :, :].rearrange("p b e t -> p (b e t)"),
                           ACT.Exp).then_inc(S["exp2"], 1)
            for n in range(2 * ROUNDS):
                k = n // ROUNDS
                act.wait_ge(S["keys"], k + 1)
                if n:
                    act.wait_ge(S["digits"], 2 * n)
                keys = (khi, klo)[k]
                for j in range(DV, NC):
                    last = act.activation(junk[:, j, :], keys[:, :], ACT.Sign, bias=cur[:, k, j:j + 1], scale=-1.0,
                                          accum_out=cnt[:, j:j + 1])
                last.then_inc(S["acounts"], 1)

            def a_xt(j, k):
                act.wait_ge(S["xt_ready"], j + 1)
                act.copy(xt[:, k % 2, :], (pT, pF)[k % 2][:, 0:P]).then_inc(S["xt_done"], 1)

            def a_w(j, k):
                e = act.value_load(eid[0:1, j], min_val=0, max_val=E - 1)
                act.copy(wcur[:, k:k + 1, :], ew[:, bass.ds(e, 1), 0:F]).then_inc(S["w_done"], 1)

            def a_gelu(j, k):
                act.wait_ge(S["up_ready"], j + 1)
                act.activation(eh[:, k % 2, :], pH[k % 2][:, 0:F], ACT.Gelu).then_inc(S["eh_done"], 1)

            act.wait_ge(S["slots_done"], 1)
            act.wait_ge(S["ld_moe"], 48)
            a_w(slice(0, 1), 0)
            a_xt(0, 0)
            a_w(slice(1, 2), 1)
            a_gelu(0, 0)
            a_xt(1, 1)
            a_w(slice(2, 3), 2)
            with act.Fori(0, NL // R) as i:
                for k in range(R):
                    a_gelu(i * R + (k + 1), k + 1)
                    a_xt(i * R + (k + 2), k + 2)
                    a_w(bass.ds(i * R + (k + 3), 1), (k + 3) % RW)
            for j in range(NL, NJ - 1):
                a_gelu(j + 1, j + 1)
                if j + 2 < NJ:
                    a_xt(j + 2, j + 2)
                if j + 3 < NJ:
                    a_w(slice(j + 3, j + 4), (j + 3) % RW)

        @block.tensor
        def _(te):
            te.wait_ge(S["consts"], 1)
            te.wait_ge(S["silu_done"], 1)
            te.wait_ge(S["ld_mod"], 16)
            for n, j in enumerate((0, 1, 3, 4)):
                mm = te.matmul(pG[:, 2 * n:2 * n + 2], wmod_sb[:, j * D:(j + 1) * D], siluT[:, :], start=True, stop=True)
            mm.then_inc(S["mod_cols"], 1)
            te.wait_ge(S["silu_done"], 2)

            def p_tx(g):
                te.wait_ge(S["xn1"], g + 1)
                if g >= 1:
                    te.wait_ge(S["hT_done"], g)
                for t in range(GT):
                    mm = te.transpose(pT[:, t * P:(t + 1) * P], xn[:, g, t, :], ident[:, :])
                mm.then_inc(S["tx"], 1)

            def p_q(g):
                te.wait_ge(S["hT_done"], g + 1)
                if g >= 2:
                    te.wait_ge(S["feat_done"], g - 1)
                te.matmul(pQ[g % 2][:, :], wq[:, :], hT[:, g % 2, :], start=True, stop=True).then_inc(S["q_ready"], 1)

            def p_tf(g):
                te.wait_ge(S["feat_done"], g + 1)
                if g >= 1:
                    te.wait_ge(S["ft_done"], g)
                for t in range(GT):
                    mm = te.transpose(pF[:, t * P:(t + 1) * P], featT[:, (g * GT + t) * P:(g * GT + t + 1) * P], ident[:, :])
                mm.then_inc(S["tf"], 1)

            def p_gt(g):
                b = g // GB
                te.wait_ge(S["ft_done"], g + 1)
                for t in range(GT):
                    mm = te.matmul(pGL[b][:, 0:P], xn[:, g, t, :], feat[:, g * GT + t, :],
                                   start=(g % GB == 0 and t == 0), stop=(g % GB == GB - 1 and t == GT - 1))
                mm.then_inc(S["gt_done"], 1)

            def p_kv(b):
                te.wait_ge(S["gts_done"], b + 1)
                te.wait_ge(S["ks_done"], b + 1)
                te.wait_ge(S["rows_read"], 1)
                te.matmul(pH0[:, 0:P], wqm[:, b, :], gts[:, b, :], start=True, stop=False)
                te.matmul(pH0[:, 0:P], qbias[:, b, :], kdiag[:, b, :], start=False, stop=True).then_inc(S["kv_ready"], 1)
                te.wait_ge(S["kvt_done"], b + 1)
                if b:
                    te.wait_ge(S["mall_done"], b)
                te.matmul(pH1[:, 0:D + F], kvt[:, b, :], wmx[:, :], start=True, stop=True).then_inc(S["mall_ready"], 1)

            for s in range(G + 3):
                if s < G:
                    p_tx(s)
                if s == 0:
                    for b in range(B):
                        te.matmul(pH[b][:, 0:512], siluB[:, b, :], wmod_sb[:, 0:512], start=True, stop=True)
                    for b in range(B):
                        mm = te.matmul(pL[:, b * 256:(b + 1) * 256], siluB[:, b, :], wmod_sb[:, 512:768], start=True, stop=True)
                    mm.then_inc(S["mod_rows"], 1)
                if s == 1:
                    te.wait_ge(S["ld_attn"], 16 * 9)
                if 0 <= s - 1 < G:
                    p_q(s - 1)
                if 0 <= s - 2 < G:
                    p_tf(s - 2)
                if 0 <= s - 3 < G:
                    if s - 3 == GB:
                        te.wait_ge(S["rows_read"], 1)
                    p_gt(s - 3)
                if s == 5:
                    te.wait_ge(S["rows_read"], 1)
                    te.transpose(pH0[:, 0:P], wm[:, :], ident[:, :]).then_inc(S["wmT_ready"], 1)
                    for b in range(B):
                        mm = te.matmul(pH1[:, b * P:(b + 1) * P], saB[:, b, :], wq[:, :], start=True, stop=True)
                    mm.then_inc(S["qb_ready"], 1)
                if s == 6:
                    te.wait_ge(S["wmT_done"], 1)
                    te.matmul(pH0[:, 0:F], wmT[:, :], w1[:, :], start=True, stop=True).then_inc(S["wmw1_ready"], 1)
                if s == GB + 3:
                    te.wait_ge(S["prep_done"], 1)
                    te.wait_ge(S["wmx_done"], 1)
                    p_kv(0)

            def p_den(g):
                b = g // GB
                if g >= 1:
                    te.wait_ge(S["z_done"], g)
                for t in range(GT):
                    mm = te.matmul(pG[:, t * H:(t + 1) * H], featT[:, (g * GT + t) * P:(g * GT + t + 1) * P],
                                   ksel[:, b, :], start=True, stop=True)
                mm.then_inc(S["den_ready"], 1)

            def p_tq(g):
                te.wait_ge(S["qp_done"], g + 1)
                if g >= 1:
                    te.wait_ge(S["qT_done"], g)
                for t in range(GT):
                    mm = te.transpose(pF[:, t * P:(t + 1) * P], qp[:, g % 2, t * P:(t + 1) * P], ident[:, :])
                mm.then_inc(S["tq"], 1)

            def p_y1(g):
                b = g // GB
                te.wait_ge(S["qT_done"], g + 1)
                if g % GB == 0:
                    te.wait_ge(S["mall_done"], b + 1)
                if g >= 1:
                    te.wait_ge(S["u1_done"], g)
                for t in range(GT):
                    mm = te.matmul(pQ0[:, t * D:(t + 1) * D], qT[:, g % 2, t * P:(t + 1) * P], mall[:, b, 0:D],
                                   start=True, stop=True)
                mm.then_inc(S["y1_ready"], 1)
                if g == 0:
                    te.wait_ge(S["mall_done"], B)
                if g >= 1:
                    te.wait_ge(S["relu0"], g)
                    te.wait_ge(S["relu1"], g)
                for f in range(2):
                    mm = te.matmul(pH[f][:, :], mall[:, b, D + f * P:D + (f + 1) * P], qT[:, g % 2, :], start=True, stop=True)
                mm.then_inc(S["m1_ready"], 1)

            def p_y2(g):
                te.wait_ge(S["relu0"], g + 1)
                te.wait_ge(S["relu1"], g + 1)
                if g >= 1:
                    te.wait_ge(S["u2_done"], g)
                for t in range(GT):
                    for f in range(2):
                        mm = te.matmul(pQ1[:, t * D:(t + 1) * D], hid[:, g % 2, f, t * P:(t + 1) * P], w2[:, f, :],
                                       start=(f == 0), stop=(f == 1))
                mm.then_inc(S["y2_ready"], 1)

            def p_tx3(g):
                te.wait_ge(S["xn3"], g + 1)
                if g >= 1:
                    te.wait_ge(S["h2_done"], g)
                for t in range(GT):
                    mm = te.transpose(pT[:, t * P:(t + 1) * P], xn[:, g, t, :], ident[:, :])
                mm.then_inc(S["tx3"], 1)

            def p_lg(g):
                te.wait_ge(S["h2_done"], g + 1)
                for t in range(GT):
                    k = g * GT + t
                    mm = te.matmul(pL[:, k * E:(k + 1) * E], h2T[:, g % 2, t * P:(t + 1) * P], wg[:, :], start=True, stop=True)
                mm.then_inc(S["lg_ready"], 1)

            for s in range(G + 8):
                if s < G:
                    p_den(s)
                if 0 <= s - 1 < G:
                    p_tq(s - 1)
                if s == 1:
                    p_kv(1)
                if 0 <= s - 6 < G:
                    p_tx3(s - 6)
                if 0 <= s - 2 < G:
                    p_y1(s - 2)
                if 0 <= s - 3 < G:
                    p_y2(s - 3)
                if 0 <= s - 7 < G:
                    p_lg(s - 7)

            te.wait_ge(S["probs"], 1)
            for b in range(B):
                mm = te.transpose(pT[:, b * P:(b + 1) * P], pr[:, b, :, :].rearrange("p e t -> p (e t)"), ident[:, :])
            mm.then_inc(S["prt_ready"], 1)
            for n in range(2 * ROUNDS):
                if n:
                    te.wait_ge(S["digits"], 2 * n)
                te.matmul(pG[:, DV - 1:NC - 1], ones[:, :], c16[:, :], start=True, stop=False, skip_group_check=True)
                te.wait_ge(S["acounts"], n + 1)
                te.matmul(pG[:, DV - 1:NC - 1], half16[:, :], cnt[:, DV:NC], start=False, stop=True, skip_group_check=True)
                te.wait_ge(S["counts"], n + 1)
                te.matmul(pG[:, 0:DV - 1], same16[:, :], cnt[:, 1:DV], start=True, stop=True,
                          skip_group_check=True).then_inc(S["totals"], 1)
            te.wait_ge(S["diagT"], 1)
            te.matmul(pG[:, 0:P], ones[:, :], thd[:, :], start=True, stop=True).then_inc(S["thr_ready"], 1)
            te.wait_ge(S["gt_ready"], 1)
            te.matmul(pF[:, 0:B * P], onesb[:, :], gt_b[:, :, :, :].rearrange("p b e t -> p (b e t)"),
                      start=True, stop=True).then_inc(S["cgt_ready"], 1)
            te.wait_ge(S["rsum_ready"], 1)
            te.matmul(pL[:, 0:B * E], before[:, :], rsum[:, :, :].rearrange("p b e -> p (b e)"), start=True, stop=False,
                      skip_group_check=True)
            te.matmul(pL[:, E:2 * E], onesb[:, :], rsum[:, 0, :], start=False, stop=True,
                      skip_group_check=True).then_inc(S["base_ready"], 1)

            te.wait_ge(S["rank_ready"], 1)
            te.matmul(pL[:, 0:B * E], before[:, :], rsum[:, :, :].rearrange("p b e -> p (b e)"), start=True, stop=False,
                      skip_group_check=True)
            te.matmul(pL[:, E:2 * E], onesb[:, :], rsum[:, 0, :], start=False, stop=True, skip_group_check=True)
            for b in range(B):
                mm = te.matmul(pL[:, 2 * E:3 * E], onesb[:, :], rsum[:, b, :], start=(b == 0), stop=(b == B - 1),
                               skip_group_check=True)
            mm.then_inc(S["rbase_ready"], 1)
            for t in range(NT):
                q = t // (NT // 4)
                te.wait_ge(S["hi_ready"], q + 1)
                if q >= POOLQ:
                    te.wait_ge(S["lo_ready"], q - POOLQ + 1)
                mm = te.matmul(pG[:, 0:2 * NJ], ohlo[:, t, :], ohi[:, t, :, :].rearrange("p v j -> p (v j)"),
                               start=(t == 0), stop=(t == NT - 1))
            mm.then_inc(S["inv_ready"], 1)

            def p_xt(j, n, k):
                te.wait_ge(gathered[k % R], n)
                te.transpose((pT, pF)[k % 2][:, 0:P], row[:, k % R, 0:D], ident[:, :]).then_inc(S["xt_ready"], 1)

            def p_up(j, k):
                te.wait_ge(S["w_done"], j + 1)
                te.wait_ge(S["xt_done"], j + 1)
                for f in range(2):
                    mm = te.matmul(pH[k % 2][:, f * P:(f + 1) * P], wcur[:, k % RW, f * P:(f + 1) * P], xt[:, k % 2, :],
                                   start=True, stop=True)
                mm.then_inc(S["up_ready"], 1)

            def p_down(j, js, k):
                e = te.value_load(eid[0:1, js], min_val=0, max_val=E - 1)
                te.wait_ge(S["eh_done"], j + 1)
                te.wait_ge(S["y_free"], j + 1)
                for f in range(2):
                    mm = te.matmul(pQ[k % 2][:, 0:D], eh[:, k % 2, f * P:(f + 1) * P], ew[:, bass.ds(e, 1), F + f * D:F + (f + 1) * D],
                                   start=(f == 0), stop=(f == 1))
                mm.then_inc(S["y_ready"], 1)

            te.wait_ge(S["ld_moe"], 48)
            p_xt(0, 16, 0)
            p_up(0, 0)
            p_xt(1, 16, 1)
            te.wait_ge(S["ohw_ready"], 1)
            for t in range(NT):
                mm = te.matmul(pL[:, 0:3 * NJ], ohlo[:, t, :], ohw[:, t, :, :].rearrange("p v j -> p (v j)"),
                               start=(t == 0), stop=(t == NT - 1))
            mm.then_inc(S["inv_ready"], 1)
            with te.Fori(0, NL // R) as i:
                for k in range(R):
                    p_up(i * R + (k + 1), k + 1)
                    p_xt(i * R + (k + 2), i * 16 + (16 if k < R - 2 else 32), k + 2)
                    p_down(i * R + k, bass.ds(i * R + k, 1), k)
            for j in range(NL, NJ):
                if j + 1 < NJ:
                    p_up(j + 1, j + 1)
                if j + 2 < NJ:
                    p_xt(j + 2, 16 * ((j + 2) // R + 1), j + 2)
                p_down(j, slice(j, j + 1), j)

        @block.vector
        def _(dve):
            n = 0

            def link(ins):
                nonlocal n
                n += 1
                ins.then_inc(S["dve"], 1)
                dve.wait_ge(S["dve"], n)

            def stats(g, ready):
                for t in range(GT):
                    last = dve.bn_stats(bn[:, g, t, :], x_sb[:, g * GT + t, :])
                link(last)
                for t in range(GT):
                    last = dve.bn_aggr(mv[:, g, t, :], bn[:, g, t, :])
                return last.then_inc(S[ready], 1)

            def normalise(g):
                for t in range(GT):
                    last = dve.tensor_scalar(xn[:, g, t, :], x_sb[:, g * GT + t, :], mv[:, g, t, 0:1],
                                             rs[:, g, t:t + 1], ALU.subtract, ALU.mult)
                return last

            def v_stats1(g):
                dve.wait_ge(ld_x[g], 16)
                stats(g, "stats1")

            def v_xn1(g):
                dve.wait_ge(S["rs1"], g + 1)
                normalise(g).then_inc(S["xn1"], 1)

            def v_feat(g):
                dve.wait_ge(S["exp_done"], g + 1)
                dve.scalar_tensor_tensor(featT[:, g * W:(g + 1) * W], pQ[g % 2][:, :], 0.0, ex[:, g % 2, :], ALU.max, ALU.add,
                                         accum_out=ksp[:, g:g + 1]).then_inc(S["feat_done"], 1)

            v_stats1(0)
            v_stats1(1)
            dve.wait_ge(S["consts"], 1)
            dve.wait_ge(S["silu_exp"], 1)
            link(dve.tensor_scalar(ec[:, :], ec[:, :], 1.0, None, ALU.add))
            link(dve.reciprocal(ec[:, :], ec[:, :]))
            dve.wait_ge(S["ld_c"], 16)
            dve.tensor_tensor(siluT[:, :], cT[:, :], ec[:, :], ALU.mult).then_inc(S["silu_done"], 1)
            dve.wait_ge(S["silu_done"], 1)
            v_xn1(0)
            for b in range(B):
                last = dve.tensor_scalar(siluB[:, b, :], ones[:, :], siluT[:, b:b + 1], None, ALU.mult)
            last.then_inc(S["silu_done"], 1)
            dve.wait_ge(S["mod_cols"], 1)
            link(dve.tensor_copy(colm[:, :, :].rearrange("p j b -> p (j b)"), pG[:, 0:8]))
            dve.tensor_scalar(colm[:, 1, :], colm[:, 1, :], 1.0, None, ALU.add)
            link(dve.tensor_scalar(colm[:, 3, :], colm[:, 3, :], 1.0, None, ALU.add))
            dve.tensor_scalar(saB[:, 0, :], ones[:, :], colm[:, 0, 0:1], None, ALU.mult)
            dve.tensor_scalar(saB[:, 1, :], ones[:, :], colm[:, 0, 1:2], None, ALU.mult).then_inc(S["cols_ready"], 1)
            dve.wait_ge(S["cols_ready"], 1)
            v_xn1(1)
            v_stats1(2)

            def prep_weights():
                dve.wait_ge(S["ld_attn"], 16 * 9)
                dve.wait_ge(S["wmT_ready"], 1)
                dve.tensor_copy(wmT[:, :], pH0[:, 0:P]).then_inc(S["wmT_done"], 1)
                dve.reduce_sum(rowm[:, 0:1], wm[:, :], AX.X)
                link(dve.reduce_sum(rowm[:, 1:3], w2[:, :, :], AX.X))
                link(dve.tensor_scalar(rowm[:, 0:3], rowm[:, 0:3], -1.0 / D, None, ALU.mult))
                dve.tensor_scalar(wmx[:, 0:D], wm[:, :], rowm[:, 0:1], None, ALU.add)
                for k in range(2):
                    dve.tensor_scalar(w2[:, k, :], w2[:, k, :], rowm[:, 1 + k:2 + k], None, ALU.add)
                for b in range(B):
                    dve.tensor_scalar(wqm[:, b, :], wq[:, :], colm[:, 1, b:b + 1], None, ALU.mult)
                dve.wait_ge(S["qb_ready"], 1)
                dve.tensor_copy(qbias[:, :, :].rearrange("p b d -> p (b d)"), pH1[:, 0:2 * P]).then_inc(S["prep_done"], 1)

            def prep_wmw1():
                dve.wait_ge(S["wmw1_ready"], 1)
                dve.tensor_copy(wmx[:, D:D + F], pH0[:, 0:F]).then_inc(S["wmx_done"], 1)

            def clamp(dst, v):
                link(dve.tensor_scalar(sgn[:, :, :], v, 0.0, 2.0, ALU.is_ge, ALU.mult))
                link(dve.scalar_tensor_tensor(dst, sgn[:, :, :], 1.0, v, ALU.subtract, ALU.mult))
                link(dve.tensor_scalar(dst, dst, 0.25, None, ALU.max))
                link(dve.scalar_tensor_tensor(dst, sgn[:, :, :], 1.0, dst, ALU.subtract, ALU.mult))

            def prep_rows():
                dve.wait_ge(S["ld_attn"], 16 * 9)
                link(dve.tensor_tensor(bsum[:, :], rows[:, 1, :], rows[:, 3, :], ALU.add))

                dve.wait_ge(S["rows_read"], 1)
                clamp(gaR[:, :, :], modr[:, :, 2 * D:3 * D])
                link(dve.tensor_tensor(rD[:, :, :], modr[:, :, 0:D], bsum[:, :].unsqueeze(1).to_broadcast([P, B, D]), ALU.add))
                link(dve.tensor_tensor(rD[:, :, :], rD[:, :, :], gaR[:, :, :], ALU.mult))
                dve.scalar_tensor_tensor(rA[:, :, :], modr[:, :, D:2 * D], 1.0, gaR[:, :, :], ALU.add, ALU.mult)\
                   .then_inc(S["rows_done"], 1)
            def prep_gb():
                for dst, n in ((rB, 0), (rC, 2)):
                    last = dve.tensor_tensor(dst[:, :, :], rows[:, n, :].unsqueeze(1).to_broadcast([P, B, D]), gaR[:, :, :],
                                             ALU.mult)
                last.then_inc(S["rows_done"], 1)
                clamp(gbR[:, :, :], modr[:, :, 4 * D:5 * D])
                dve.tensor_tensor(dgb[:, :], gbR[:, 1, :], gbR[:, 0, :], ALU.subtract)

            def v_ksum(b):
                dve.wait_ge(S["feat_done"], GB * (b + 1))
                link(dve.reduce_sum(ksum[:, b:b + 1], ksp[:, b * GB:(b + 1) * GB], AX.X))
                dve.tensor_scalar(ksel[:, b, :], same16[:, 0:P:HD], ksum[:, b:b + 1], None, ALU.mult)
                dve.tensor_scalar(kdiag[:, b, :], ident[:, :], ksum[:, b:b + 1], None, ALU.mult).then_inc(S["ks_done"], 1)

            def v_kvt(b):
                dve.wait_ge(S["kv_ready"], b + 1)
                dve.tensor_tensor(kvt[:, b, :], pH0[:, 0:P], same16[:, :], ALU.mult).then_inc(S["kvt_done"], 1)

            for s in range(G + 1):
                if 0 <= s - 1 < G:
                    v_feat(s - 1)
                if s + 3 < G:
                    v_stats1(s + 3)
                if s + 2 < G:
                    v_xn1(s + 2)
                if s == 1:
                    prep_rows()
                if s == 6:
                    prep_weights()
                if s == 7:
                    prep_wmw1()
                if s == GB + 1:
                    v_ksum(0)
                if s == G:
                    prep_gb()
                if s == GB + 3:
                    v_kvt(0)
            v_ksum(1)

            def v_z(g):
                dve.wait_ge(S["den_ready"], g + 1)
                if g >= 2:
                    dve.wait_ge(S["qp_done"], g - 1)
                link(dve.tensor_scalar(z[:, g % 2, :], pG[:, 0:GT * H], ATTN_EPS, None, ALU.add))
                dve.reciprocal(z[:, g % 2, :], z[:, g % 2, :]).then_inc(S["z_done"], 1)

            def v_relu(g):
                dve.wait_ge(S["m1_ready"], g + 1)
                if g >= 2:
                    dve.wait_ge(S["y2_ready"], g - 1)
                dve.tensor_scalar(hid[:, g % 2, 1, :], pH1[:, :], 0.0, None, ALU.max).then_inc(S["relu1"], 1)

            def v_u1(g):
                dve.wait_ge(S["sq1"], g + 1)
                dve.tensor_tensor(u1[:, g % 3], pQ0[:, :].rearrange("p (t d) -> p t d", d=D), row4(rB[:, g // GB, :]),
                                  ALU.mult).then_inc(S["u1_done"], 1)

            def v_u2(g):
                dve.wait_ge(S["sq2"], g + 1)
                dve.tensor_tensor(u2[:, g % 2], pQ1[:, :].rearrange("p (t d) -> p t d", d=D), row4(rC[:, g // GB, :]),
                                  ALU.mult).then_inc(S["u2_done"], 1)

            def v_x1(g):
                dve.wait_ge(S["yr_done"], g + 1)
                dve.wait_ge(S["acc_done"], g + 1)
                for u, n in ((u1[:, g % 3], 0), (u2[:, g % 2], GT)):
                    for t in range(GT):
                        x1 = x_sb[:, g * GT + t, :]
                        last = dve.scalar_tensor_tensor(x1, u[:, t, :], yr[:, g % 2, n + t:n + t + 1], x1, ALU.mult, ALU.add)
                    if n == 0:
                        link(last)
                last.then_inc(S["x1_done"], 1)
                dve.wait_ge(S["x1_done"], g + 1)
                stats(g, "stats3")

            def v_xn3(g):
                dve.wait_ge(S["rs3"], g + 1)
                if g == 0:
                    dve.wait_ge(S["gt_done"], G)
                normalise(g).then_inc(S["xn3"], 1)

            for s in range(G + 6):
                if s < G:
                    v_z(s)
                if s == 1:
                    v_kvt(1)
                if 0 <= s - 5 < G:
                    v_xn3(s - 5)
                if 0 <= s - 4 < G:
                    v_x1(s - 4)
                if 0 <= s - 2 < G:
                    v_relu(s - 2)
                if 0 <= s - 2 < G:
                    v_u1(s - 2)
                if 0 <= s - 3 < G:
                    v_u2(s - 3)

            def flat(t):
                return t[:, :, :, :].rearrange("p b e t -> p (b e t)")

            def over_e(t, op, src):
                return dve.tensor_reduce(t, src.rearrange("p b e t -> p b t e"), AX.X, op)

            def b_et(t):
                return t[:, :, :].unsqueeze(2).to_broadcast([P, B, E, TB])

            def be_(t):
                return t[:, :, :].unsqueeze(3).to_broadcast([P, B, E, TB])

            dve.wait_ge(S["lg_ready"], G)
            lg = pL[:, 0:NT * E].rearrange("p (b t e) -> p b e t", b=B, e=E)
            link(over_e(mx[:, :, :], ALU.max, lg))
            for b in range(B):
                last = dve.tensor_tensor(m1[:, b], lg[:, b], mx[:, b, :].unsqueeze(1).to_broadcast([P, E, TB]), ALU.subtract)
            last.then_inc(S["lmax"], 1)
            dve.wait_ge(S["exp2"], 1)
            link(over_e(sm[:, :, :], ALU.add, pe_[:, :, :, :]))
            link(dve.reciprocal(sm[:, :, :], sm[:, :, :]))
            for b in range(B):
                last = dve.tensor_tensor(pr[:, b], pe_[:, b], sm[:, b, :].unsqueeze(1).to_broadcast([P, E, TB]), ALU.mult)
            last.then_inc(S["probs"], 1)
            dve.wait_ge(S["prt_ready"], 1)
            link(dve.tensor_copy(prT[:, :], pT[:, 0:B * P]))
            bits = prT[:, :].bitcast(I32)
            link(dve.tensor_scalar(ki[:, :], bits, HALF, None, ALU.logical_shift_right))
            link(dve.tensor_copy(khi[:, :], ki[:, :]))
            link(dve.tensor_scalar(ki[:, :], bits, (1 << HALF) - 1, None, ALU.bitwise_and))
            link(dve.tensor_copy(klo[:, :], ki[:, :]))

            def search(keys, k):
                dve.tensor_scalar(cur[:, k, :], jc[:, :], steps[:, 0:1], -0.5, ALU.mult, ALU.add).then_inc(S["keys"], 1)
                dve.wait_ge(S["keys"], k + 1)
                for r in range(ROUNDS):
                    n = k * ROUNDS + r
                    if n:
                        dve.wait_ge(S["totals"], n)
                    for j in range(1, DV):
                        last = dve.tensor_scalar(junk[:, j, :], keys, cur[:, k, j:j + 1], None, ALU.is_ge, ALU.add,
                                                 accum_out=cnt[:, j:j + 1])
                    last.then_inc(S["counts"], 1)
                    dve.scalar_tensor_tensor(pre[:, :], jc[:, :], steps[:, r + 1:r + 2],
                                             cur[:, k, 0:1].to_broadcast([P, NC]), ALU.mult, ALU.add)
                    dve.wait_ge(S["totals"], n + 1)
                    dve.tensor_scalar(dig[:, :], pG[:, 0:NC - 1], CAP - 0.5, None, ALU.is_ge, ALU.add,
                                      accum_out=digit[:, :]).then_inc(S["digits"], 1)
                    dve.wait_ge(S["digits"], 2 * n + 1)
                    dve.scalar_tensor_tensor(cur[:, k, :], digit[:, 0:1].to_broadcast([P, NC]),
                                             steps[:, r:r + 1], pre[:, :], ALU.mult, ALU.add).then_inc(S["digits"], 1)
                    dve.wait_ge(S["digits"], 2 * n + 2)

            search(khi[:, :], 0)
            link(dve.tensor_scalar(thr0[:, :], cur[:, 0, 0:1], 0.5, None, ALU.add))
            link(dve.tensor_scalar(khi[:, :], khi[:, :], thr0[:, 0:1], 65536.0, ALU.subtract, ALU.mult))
            link(dve.tensor_tensor(klo[:, :], khi[:, :], klo[:, :], ALU.add))
            search(klo[:, :], 1)
            link(dve.tensor_scalar(thi[:, :], cur[:, :, 0], 0.5, None, ALU.add))
            link(dve.tensor_scalar(thi[:, 0:1], thi[:, 0:1], HALF, None, ALU.logical_shift_left))
            link(dve.tensor_tensor(thi[:, 0:1], thi[:, 0:1], thi[:, 1:2], ALU.bitwise_or))
            dve.tensor_scalar(thd[:, :], ident[:, :], thi[:, 0:1].bitcast(F32), None, ALU.mult).then_inc(S["diagT"], 1)
            dve.wait_ge(S["thr_ready"], 1)
            link(dve.tensor_copy(thr[:, :], pG[:, 0:P]))
            tb = thr[:, :].unsqueeze(1).to_broadcast([P, B, P])
            pf = pr[:, :, :, :].rearrange("p b e t -> p b (e t)")
            dve.tensor_tensor(gt_b[:, :, :, :].rearrange("p b e t -> p b (e t)"), pf, tb, ALU.is_gt).then_inc(S["gt_ready"], 1)
            link(dve.tensor_tensor(eq[:, :, :, :].rearrange("p b e t -> p b (e t)"), pf, tb, ALU.is_equal))
            link(dve.tensor_tensor_scan(flat(scan), segmask[:, :], flat(eq), 0.0, ALU.mult, ALU.add))
            dve.tensor_copy(rsum[:, :, :], scan[:, :, :, TB - 1]).then_inc(S["rsum_ready"], 1)
            dve.wait_ge(S["rsum_ready"], 1)
            link(dve.tensor_tensor(flat(scan), flat(scan), flat(eq), ALU.subtract))
            dve.wait_ge(S["cgt_ready"], 1)
            link(dve.tensor_reduce(base[:, :, :], pF[:, 0:B * P].rearrange("p (b e t) -> p b e t", b=B, e=E), AX.X, ALU.add))
            link(dve.tensor_tensor(cgt[:, :], base[:, 0, :], base[:, 1, :], ALU.add))
            dve.wait_ge(S["base_ready"], 1)
            link(dve.tensor_tensor(base[:, :, :], pL[:, 0:B * E].rearrange("p (b e) -> p b e", b=B),
                                   cgt[:, :].unsqueeze(1).to_broadcast([P, B, E]), ALU.add))
            link(dve.tensor_tensor(m1[:, :, :, :], scan[:, :, :, :], be_(base), ALU.add))
            link(dve.scalar_tensor_tensor(flat(m2), flat(m1), CAP - 0.5, flat(eq), ALU.is_lt, ALU.mult))
            link(dve.tensor_tensor(flat(sel), flat(m2), flat(gt_b), ALU.add))
            link(over_e(anys[:, :, :], ALU.max, sel[:, :, :, :]))
            for b in range(B):
                last = dve.scalar_tensor_tensor(m1[:, b], sel[:, b], 1.0, anys[:, b, :].unsqueeze(1).to_broadcast([P, E, TB]),
                                                ALU.subtract, ALU.mult)
            link(last)
            link(dve.scalar_tensor_tensor(flat(m1), flat(m1), 2.0, flat(pr), ALU.mult, ALU.add))
            link(over_e(mx[:, :, :], ALU.max, m1[:, :, :, :]))
            link(dve.tensor_tensor(m2[:, :, :, :], m1[:, :, :, :], b_et(mx), ALU.is_lt))
            for b in range(B):
                last = dve.scalar_tensor_tensor(m2[:, b], m2[:, b], float(E), eidx[:, :].unsqueeze(2).to_broadcast([P, E, TB]),
                                                ALU.mult, ALU.add)
            link(last)
            link(over_e(sm[:, :, :], ALU.min, m2[:, :, :, :]))
            link(dve.tensor_tensor(m1[:, :, :, :], m2[:, :, :, :], b_et(sm), ALU.is_equal))
            oh = m1
            link(dve.tensor_tensor_scan(flat(scan), segmask[:, :], flat(oh), 0.0, ALU.mult, ALU.add))
            dve.tensor_copy(rsum[:, :, :], scan[:, :, :, TB - 1]).then_inc(S["rank_ready"], 1)
            wt = mx[:, :, :].rearrange("p b t -> p (b t)")
            dve.wait_ge(S["rbase_ready"], 1)
            link(dve.tensor_copy(tot[:, :], pL[:, 2 * E:3 * E]))
            link(dve.tensor_scalar(toti[:, :], tot[:, :], float(P - 1), None, ALU.add))
            link(dve.tensor_scalar(toti[:, :], toti[:, :], 7, None, ALU.logical_shift_right))
            link(dve.tensor_copy(ntile[:, :], toti[:, :]))
            link(dve.tensor_tensor_scan(tend[:, :], ones[:, 0:E], ntile[:, :], 0.0, ALU.mult, ALU.add))
            link(dve.tensor_tensor(tot[:, :], tend[:, :], ntile[:, :], ALU.subtract))
            for b in range(B):
                last = dve.scalar_tensor_tensor(base[:, b, :], tot[:, :], float(P), pL[:, b * E:(b + 1) * E], ALU.mult, ALU.add)
            link(last)
            link(dve.tensor_tensor(m2[:, :, :, :], scan[:, :, :, :], be_(base), ALU.add))
            link(dve.tensor_tensor(flat(m2), flat(m2), flat(oh), ALU.mult))
            link(over_e(sm[:, :, :], ALU.add, m2[:, :, :, :]))
            link(dve.tensor_scalar(posi[:, :], sm[:, :, :].rearrange("p b t -> p (b t)"), -1.0, None, ALU.add))
            dve.tensor_scalar(loi[:, :], posi[:, :], P - 1, None, ALU.bitwise_and)
            link(dve.tensor_scalar(hii[:, :], posi[:, :], 7, None, ALU.logical_shift_right))
            dve.tensor_copy(lo[:, :], loi[:, :])
            dve.tensor_copy(hi[:, :], hii[:, :]).then_inc(S["slot_ready"], 1)
            dve.wait_ge(S["slot_ready"], 1)
            nq = NT // 4
            for q in range(4):
                ts = slice(q * nq, (q + 1) * nq)
                if q < POOLQ:
                    dve.tensor_tensor(ohlo[:, ts, :], iota[:, :].unsqueeze(1).to_broadcast([P, nq, P]),
                                      lo[:, ts].unsqueeze(2).to_broadcast([P, nq, P]), ALU.is_equal)
                link(dve.tensor_tensor(ohhi[:, ts, :], iotaj[:, 0:NJ].unsqueeze(1).to_broadcast([P, nq, NJ]),
                                       hi[:, ts].unsqueeze(2).to_broadcast([P, nq, NJ]), ALU.is_equal))
                for v in range(2):
                    last = dve.tensor_tensor(ohi[:, ts, v, :], ohhi[:, ts, :],
                                             val[:, v, ts].unsqueeze(2).to_broadcast([P, nq, NJ]), ALU.mult)
                last.then_inc(S["hi_ready"], 1)
            link(dve.tensor_tensor(ecmp[:, :, :], iotaj[:, :].unsqueeze(2).to_broadcast([P, NJ, E]),
                                   tend[:, :].unsqueeze(1).to_broadcast([P, NJ, E]), ALU.is_ge))
            link(dve.tensor_reduce(eidf[:, :], ecmp[:, :, :], AX.X, ALU.add))
            link(dve.tensor_scalar(eid[:, :], eidf[:, :], float(E - 1), None, ALU.min))
            dve.wait_ge(S["inv_ready"], 1)
            link(dve.tensor_copy(inv[:, 0:2, :].rearrange("p v j -> p (v j)"), pG[:, 0:2 * NJ]))
            link(dve.scalar_tensor_tensor(idf[:, :], inv[:, 0, :], -1.0, inv[:, 1, :], ALU.add, ALU.add))
            dve.tensor_scalar(gidx[:, :], idf[:, :], 0.0, None, ALU.max)
            link(dve.tensor_scalar(oob[:, :], idf[:, :], 0.0, float(2 * B * L), ALU.is_lt, ALU.mult))
            dve.tensor_tensor(sidx[:, :], idf[:, :], oob[:, :], ALU.add).then_inc(S["slots_done"], 1)
            dve.tensor_scalar(flag[:, :], idf[:, :], float(L), None, ALU.is_ge)
            link(dve.tensor_copy(val[:, 2, :], wt))
            link(dve.tensor_tensor(lo[:, :], wt, val[:, 2, :], ALU.subtract))
            link(dve.tensor_copy(val[:, 3, :], lo[:, :]))
            link(dve.tensor_tensor(hi[:, :], lo[:, :], val[:, 3, :], ALU.subtract))
            link(dve.tensor_copy(val[:, 4, :], hi[:, :]))
            for v in range(3):
                last = dve.tensor_tensor(ohw[:, :, v, :], ohhi[:, :, :], val[:, 2 + v, :].unsqueeze(2).to_broadcast([P, NT, NJ]),
                                         ALU.mult)
            last.then_inc(S["ohw_ready"], 1)
            dve.wait_ge(S["inv_ready"], 2)
            link(dve.tensor_copy(inv[:, 2:5, :].rearrange("p v j -> p (v j)"), pL[:, 0:3 * NJ]))
            link(dve.tensor_tensor(wslot[:, :], inv[:, 4, :], inv[:, 3, :], ALU.add))
            link(dve.tensor_tensor(wslot[:, :], wslot[:, :], inv[:, 2, :], ALU.add))
            dve.wait_ge(S["slots_done"], 1)

            def finish(j, n, js, k):
                dve.scalar_tensor_tensor(gsel[:, k % 4, :], dgb[:, :], flag[:, js], gbR[:, 0, :], ALU.mult, ALU.add)\
                   .then_inc(S["gsel_done"], 1)
                dve.wait_ge(S["y_ready"], j + 1)
                dve.wait_ge(S["gsel_done"], j + 1)
                dve.scalar_tensor_tensor(yw[:, k % 4, :], pQ[k % 2][:, 0:D], wslot[:, js], gsel[:, k % 4, :], ALU.mult, ALU.mult)\
                   .then_inc(S["y_free"], 1)
                dve.wait_ge(S["y_free"], j + 3)
                if n is not None:
                    dve.wait_ge(scattered[k % R], n)
                dve.tensor_tensor(o_sb[:, k % R, :], yw[:, k % 4, :], row[:, k % R, D:2 * D], ALU.add).then_inc(S["o_done"], 1)

            for k in range(2):
                dve.memset(dig[:, k:k + 1], 0.0).then_inc(S["y_free"], 1)
            for j in range(R):
                finish(j, None, slice(j, j + 1), j)
            with dve.Fori(1, NL // R) as i:
                for k in range(R):
                    finish(i * R + k, i * 16, bass.ds(i * R + k, 1), k)
            for j in range(NL, NJ):
                finish(j, 16 * (j // R), slice(j, j + 1), j)


_INS = ['L0_attn_x', 'L0_attn_Wq', 'L0_attn_Wm', 'L0_attn_W1', 'L0_attn_W2', 'L0_attn_g1', 'L0_attn_b1', 'L0_attn_g2',
        'L0_attn_b2', 'L0_ffn_Wg', 'L0_ffn_W1', 'L0_ffn_W2', 'L0_c', 'L0_wmod']


def kernel(**inputs):
    import numpy as _np
    import concourse.bacc as _bacc
    from concourse import mybir as _mybir
    from concourse.bass_utils import run_bass_kernel_spmd as _run

    nc = _bacc.Bacc("TRN2", target_bir_lowering=False, num_devices=1)
    arrays, args = {}, []
    for name in _INS:
        a = _np.ascontiguousarray(inputs[name])
        arrays[f"in_{name}_dram"] = a
        args.append(nc.dram_tensor(f"in_{name}_dram", a.shape, _mybir.dt.from_np(a.dtype), kind="ExternalInput").ap())
    table = nc.dram_tensor("table_dram", (B * L, 2 * D), F32, kind="Internal").ap()
    out = nc.dram_tensor("out_dram", (B, L, D), F32, kind="ExternalOutput").ap()
    build(nc, *args, table, out)
    r = _run(nc, [arrays], core_ids=[0])
    return r.results[0]["out_dram"]
```
